# Optimizing a Trainium2 kernel written in Bass

```python
import numpy as np
import jax
import jax.numpy as jnp

def _softmax(x, axis=-1):
    return jax.nn.softmax(x, axis=axis)

def _gelu(x):
    return jax.nn.gelu(x, approximate=True)

def _silu(x):
    return jax.nn.silu(x)

def _sigmoid(x):
    return jax.nn.sigmoid(x)

def _layernorm(x, axis=-1, eps=1e-05):
    m = jnp.mean(x, axis=axis, keepdims=True)
    v = jnp.var(x, axis=axis, keepdims=True)
    return (x - m) / jnp.sqrt(v + eps)

def _scatter_add(tgt, idx, src, axis=0):
    return tgt.at[idx].add(src)

def _segment_sum(src, seg, n):
    return jax.ops.segment_sum(src, seg, n)
kernel_name = 'mk_gnn_resnorm_d1_gnn_r8_fce729'

def setup_inputs(seed: int=0):
    np.random.seed(seed)
    _w = jnp.asarray

    def _rec_inputs():
        import jax
        import jax.numpy as jnp
        _gk = jax.random.key(seed)
        x = -8.776e-05 + 1 * jax.random.normal(jax.random.fold_in(_gk, 1), (6250, 512), jnp.float32)
        _s = jax.random.randint(jax.random.fold_in(_gk, 2), (50000,), 0, 6250, jnp.int32)
        _d = jax.random.randint(jax.random.fold_in(_gk, 3), (50000,), 0, 6250, jnp.int32)
        _loop = jnp.arange(6250, dtype=jnp.int32)
        src = jnp.concatenate([_s, _d, _loop])
        dst = jnp.concatenate([_d, _s, _loop])
        _o = jnp.argsort(dst, stable=True)
        src = src[_o]
        dst = dst[_o]
        return (x, src, dst)
    x, src, dst = _rec_inputs()

    def _L0_gnn_setup():
        import jax, jax.numpy as jnp
        import numpy as np
        N_NODES = 1250
        N_EDGES = 20000
        D_IN = 512
        D_HID = 512
        D_OUT = 512

        def _gcn_norm(edge_index, n_nodes):
            loop = jnp.arange(n_nodes, dtype=edge_index.dtype)
            src = jnp.concatenate([edge_index[0], loop])
            dst = jnp.concatenate([edge_index[1], loop])
            deg = jax.ops.segment_sum(jnp.ones_like(dst, dtype=jnp.float32), dst, num_segments=n_nodes)
            dinv = jnp.where(deg > 0, jax.lax.rsqrt(jnp.maximum(deg, 1.0)), 0.0)
            norm = dinv[src] * dinv[dst]
            return (src, dst, norm)

        def _gcn_conv(x, W, b, src, dst, norm, n_nodes):
            xw = x @ W
            msg = xw[src] * norm[:, None]
            out = jax.ops.segment_sum(msg, dst, num_segments=n_nodes)
            return out + b
        key = jax.random.key(seed)
        ks = jax.random.split(key, 8)
        x = jax.random.normal(ks[0], (N_NODES, D_IN), dtype=jnp.float32)
        edge_index = jax.random.randint(ks[1], (2, N_EDGES), 0, N_NODES, dtype=jnp.int64)

        def glorot(k, fan_in, fan_out):
            s = jnp.sqrt(6.0 / (fan_in + fan_out))
            return jax.random.uniform(k, (fan_in, fan_out), dtype=jnp.float32, minval=-s, maxval=s)
        W1 = glorot(ks[2], D_IN, D_HID)
        W2 = glorot(ks[3], D_HID, D_OUT)
        W3 = glorot(ks[4], D_OUT, D_OUT)
        b1 = jnp.zeros((D_HID,), jnp.float32)
        b2 = jnp.zeros((D_OUT,), jnp.float32)
        b3 = jnp.zeros((D_OUT,), jnp.float32)
        return {'x': x, 'edge_index': edge_index, 'W1': W1, 'b1': b1, 'W2': W2, 'b2': b2, 'W3': W3, 'b3': b3}
    _L0_gnn_all = _L0_gnn_setup()
    _L0_gnn_in = {k: v for k, v in _L0_gnn_all.items() if k in ('W1', 'b1', 'W2', 'b2', 'W3', 'b3')}
    del _L0_gnn_all
    return {'x': x, 'src': src, 'dst': dst, 'L0_gnn_W1': _L0_gnn_in['W1'], 'L0_gnn_b1': _L0_gnn_in['b1'], 'L0_gnn_W2': _L0_gnn_in['W2'], 'L0_gnn_b2': _L0_gnn_in['b2'], 'L0_gnn_W3': _L0_gnn_in['W3'], 'L0_gnn_b3': _L0_gnn_in['b3']}

def reference(x, src, dst, L0_gnn_W1, L0_gnn_b1, L0_gnn_W2, L0_gnn_b2, L0_gnn_W3, L0_gnn_b3):
    import jax
    import jax.numpy as jnp

    def _L0_gnn_ref(x, edge_index, W1, b1, W2, b2, W3, b3):
        import jax, jax.numpy as jnp
        import numpy as np
        N_NODES = 1250
        N_EDGES = 20000
        D_IN = 512
        D_HID = 512
        D_OUT = 512

        def _gcn_norm(edge_index, n_nodes):
            loop = jnp.arange(n_nodes, dtype=edge_index.dtype)
            src = jnp.concatenate([edge_index[0], loop])
            dst = jnp.concatenate([edge_index[1], loop])
            deg = jax.ops.segment_sum(jnp.ones_like(dst, dtype=jnp.float32), dst, num_segments=n_nodes)
            dinv = jnp.where(deg > 0, jax.lax.rsqrt(jnp.maximum(deg, 1.0)), 0.0)
            norm = dinv[src] * dinv[dst]
            return (src, dst, norm)

        def _gcn_conv(x, W, b, src, dst, norm, n_nodes):
            xw = x @ W
            msg = xw[src] * norm[:, None]
            out = jax.ops.segment_sum(msg, dst, num_segments=n_nodes)
            return out + b
        n = x.shape[0]
        src, dst, norm = _gcn_norm(edge_index, n)
        h = _gcn_conv(x, W1, b1, src, dst, norm, n)
        h = _gcn_conv(h, W2, b2, src, dst, norm, n)
        h = _gcn_conv(h, W3, b3, src, dst, norm, n)
        return h
    edge_index = jnp.stack([src, dst])
    x = _layernorm(x + _L0_gnn_ref(x, edge_index, L0_gnn_W1, L0_gnn_b1, L0_gnn_W2, L0_gnn_b2, L0_gnn_W3, L0_gnn_b3), axis=-1)
    return x

_drawn_inputs = setup_inputs


def setup_inputs(seed=0):
    import zlib

    import numpy as np

    out = dict(_drawn_inputs(seed))
    spreads = {'L0_gnn_b1': (0.0, 0.1), 'L0_gnn_b2': (0.0, 0.1), 'L0_gnn_b3': (0.0, 0.1)}
    factors = {}
    for name, (base, spread) in spreads.items():
        noise = np.random.default_rng([zlib.crc32(name.encode()), seed]).standard_normal(out[name].shape)
        drawn = base * np.exp(spread * noise) if base else spread * noise
        out[name] = jnp.asarray(drawn.astype(out[name].dtype))
    for name, factor in factors.items():
        out[name] = (out[name] * factor).astype(out[name].dtype)
    return out
```

```python
from contextlib import ExitStack

import concourse.bass as bass
from concourse import mybir

F32 = mybir.dt.float32
I32 = mybir.dt.int32
BF16 = mybir.dt.bfloat16
ALU = mybir.AluOpType
ACT = mybir.ActivationFunctionType
AX = mybir.AxisListType

P = 128
EPS = 1e-5
LAYERS = 3
CPG = 4
WIN = 64
RING = 4
LAG = 5
DEG_BATCH = 16


def gcn_three_layers_resnorm(nc, x, src, dst, W1, b1, W2, b2, W3, b3, out):
    N, D = x.shape
    E = src.shape[0]
    FB = D // P
    TILES = -(-N // P)
    LAST = N - (TILES - 1) * P
    CHUNKS = -(-E // P)
    STEPS = -(-CHUNKS // (CPG * RING))
    GROUPS = STEPS * RING
    ROW_BLOCKS = -(-GROUPS * CPG // P)
    COLS = ROW_BLOCKS * P
    FULL_ROWS = E // P
    FULL_BLOCKS = FULL_ROWS // P
    TAIL_ROWS = FULL_ROWS - FULL_BLOCKS * P
    TAIL_EDGES = E - FULL_ROWS * P
    ACC_W = (TILES * P + WIN + 63) // 64 * 64
    PAIRS = (STEPS - LAG) // 2
    TILES_IN_STEPS = STEPS - LAG
    DEG_BATCHES = STEPS
    LN_STEPS = 6
    W_STEPS = 4 * FB + 4
    assert D == 512 and CPG * RING == DEG_BATCH and TILES_IN_STEPS <= TILES and (STEPS - LAG) % 2 == 1 and STEPS > LAG + 2

    y_dram = [nc.dram_tensor(f"y{l}_dram", [N, D], F32, kind="Internal").ap() for l in range(LAYERS)]

    with ExitStack() as ctx:
        def sb(name, shape, dt):
            return ctx.enter_context(nc.sbuf_tensor(name, shape, dt))

        def sem(name):
            return ctx.enter_context(nc.semaphore(name))

        acc = sb("acc", [P, FB, ACC_W], F32)
        ring = sb("ring", [P, RING * CPG, D], F32)
        onehot = sb("onehot", [P, RING, CPG, WIN], F32)
        src_idx = sb("src_idx", [P, COLS], I32)
        dst_rel = sb("dst_rel", [P, COLS], F32)
        idx_stage = sb("idx_stage", [P, RING * CPG], I32)
        base_i = sb("base_i", [1, GROUPS], I32)
        w123 = sb("w123", [P, FB, D], F32)
        w1_sb = sb("w1_sb", [P, FB, D], F32)
        w2_sb = sb("w2_sb", [P, FB, D], F32)
        w23 = sb("w23", [P, FB, D], F32)
        wT = sb("wT", [P, FB, D], F32)
        bias = sb("bias", [P, LAYERS, D], F32)
        stage = sb("stage", [P, 2, FB, P], F32)
        h_sb = sb("h_sb", [P, 2, D], F32)
        y_sb = sb("y_sb", [P, 2, D], F32)
        ident = sb("ident", [P, P], F32)
        ones = sb("ones", [P, P], F32)
        win_iota = sb("win_iota", [P, WIN], F32)
        lo_iota = sb("lo_iota", [P, P], BF16)
        hi_iota = sb("hi_iota", [P, TILES], F32)
        dinv = sb("dinv", [P, TILES], F32)
        deg = sb("deg", [P, 3, TILES], F32)
        ln = sb("ln", [P, 2, 12], F32)

        w3_sb = w123
        x_sb = w1_sb[:, 0:2, :]
        tmp = acc[:, :, :].rearrange("p f n -> p (f n)")
        cut = [0]

        def carve(words):
            cut[0] += words
            return tmp[:, cut[0] - words:cut[0]]

        src_rows = carve(COLS).bitcast(I32)
        dst_rows = carve(COLS).bitcast(I32)
        src_rows_f = carve(COLS)
        dst_rows_f = carve(COLS)
        dst_f = carve(COLS)
        dst_i = carve(COLS).bitcast(I32)
        lo_i = carve(COLS).bitcast(I32)
        hi_i = carve(COLS).bitcast(I32)
        lo_f = carve(COLS)
        hi_f = carve(COLS)
        lo_hot = carve(2 * DEG_BATCH * P // 2).bitcast(BF16).rearrange("p (b c n) -> p b c n", b=2, c=DEG_BATCH)
        hi_hot = carve(2 * DEG_BATCH * TILES // 2).bitcast(BF16).rearrange("p (b c n) -> p b c n", b=2, c=DEG_BATCH)
        hi_diff = carve(2 * DEG_BATCH * TILES // 2).bitcast(BF16).rearrange("p (b c n) -> p b c n", b=2, c=DEG_BATCH)
        b_row = carve(2 * D).rearrange("p (l d) -> p l d", l=2)
        b_cols = carve(2 * D).rearrange("p (l d) -> p l d", l=2)

        ps = ctx.enter_context(nc.psum_tensor("ps", [P, 8, 512], F32))

        consts_ready = sem("consts_ready")
        pads_ready = sem("pads_ready")
        edges_loaded = sem("edges_loaded")
        w_loaded = sem("w_loaded")
        dve_done = sem("dve_done")
        edges_turned = sem("edges_turned")
        edges_turned_in = sem("edges_turned_in")
        dst_ready = sem("dst_ready")
        deg_step = sem("deg_step")
        idx_staged = sem("idx_staged")
        hot_ready = sem("hot_ready")
        idx_done = sem("idx_done")
        base_spread = sem("base_spread")
        places_ready = sem("places_ready")
        hi_ready = sem("hi_ready")
        deg_counted = sem("deg_counted")
        sqrt_done = sem("sqrt_done")
        dinv_ready = sem("dinv_ready")
        w_step = sem("w_step")
        w_copied = sem("w_copied")
        x0_loaded = [sem(f"x0_loaded{i}") for i in range(RING * CPG)]
        y0_scaled = sem("y0_scaled")
        y0_stored = [sem(f"y0_stored{i}") for i in range(RING * CPG)]
        y0_turned = sem("y0_turned")
        acc_init = sem("acc_init")
        gathered = [sem(f"gathered{i}") for i in range(RING)]
        summed = sem("summed")
        added = sem("added")
        tile_staged = sem("tile_staged")
        tile_turned = sem("tile_turned")
        h_ready = sem("h_ready")
        y_ready = sem("y_ready")
        y_stored = [sem(f"y_stored{i}") for i in range(2)]
        y_turned = sem("y_turned")
        x_loaded = [sem(f"x_loaded{i}") for i in range(2)]
        ln_step = sem("ln_step")
        std_ready = sem("std_ready")
        o_ready = sem("o_ready")
        o_stored = [sem(f"o_stored{i}") for i in range(2)]

        XR = RING * CPG
        X_ROUNDS = (TILES - 1) // XR
        assert (TILES - 1) % XR == 0 and LAST < P

        def run_layer(eng, layer, step, tail):
            def tile(t0, m, r):
                n0 = layer * TILES + r
                return t0 + r, t0 + n0, n0 % 2, m + n0 // 2

            step(0, True, None)
            with eng.Fori(1, LAG) as i:
                step(i, False, None)
            for r in range(2):
                step(LAG + r, False, tile(0, 0, r))
            with eng.Fori(1, PAIRS) as m:
                for r in range(2):
                    step(2 * m + (LAG + r), False, tile(2 * m, m, r))
            for t in range(2 * PAIRS, TILES_IN_STEPS):
                step(t + LAG, False, tile(t // 2 * 2, t // 2, t % 2))
            for t in range(TILES_IN_STEPS, TILES):
                tail(tile(t // 2 * 2, t // 2, t % 2))

        block = ctx.enter_context(nc.Block())

        def rows_of(t):
            return LAST if isinstance(t, int) and t == TILES - 1 else P

        def node_rows(dram, t):
            return dram[bass.ds(P * t, rows_of(t)), :]

        @block.sync
        def _(sp):
            tail_at = FULL_BLOCKS * P * P
            lists = [(rows.rearrange("c (b p) -> c b p", p=P), edges) for rows, edges in ((dst_rows, dst), (src_rows, src))]
            for r3, edges in lists:
                sp.dma_start(r3[:, 0:FULL_BLOCKS, :],
                             edges[0:tail_at].rearrange("(b c p) -> c b p", c=P, p=P)).then_inc(edges_loaded, 16)
            sp.wait_ge(pads_ready, 2)
            for r3, edges in lists:
                sp.dma_start(r3[0:TAIL_ROWS, FULL_BLOCKS, :],
                             edges[tail_at:tail_at + TAIL_ROWS * P].rearrange("(c p) -> c p", p=P)
                             ).then_inc(edges_loaded, 16)
                sp.dma_start(r3[TAIL_ROWS:TAIL_ROWS + 1, FULL_BLOCKS, 0:TAIL_EDGES],
                             edges[tail_at + TAIL_ROWS * P:E].rearrange("(c p) -> c p", c=1)).then_inc(edges_loaded, 16)
            for t, w in ((w2_sb, W2), (w3_sb, W3), (w1_sb, W1)):
                sp.dma_start(t[:, :, :], w.rearrange("(k p) n -> p k n", p=P)).then_inc(w_loaded, 16)
            for l, b in enumerate((b1, b2)):
                sp.dma_start(b_row[0:1, l, :], b.rearrange("(a d) -> a d", a=1)).then_inc(w_loaded, 16)
            sp.dma_start(bias[:, 2, :], b3.rearrange("(a d) -> a d", a=1).broadcast_to([P, D])).then_inc(w_loaded, 16)

            for s in range(XR):
                sp.dma_start(ring[:, s, :], node_rows(x, s)).then_inc(x0_loaded[s], 16)
            with sp.Fori(1, X_ROUNDS) as k:
                for s in range(XR):
                    sp.wait_ge(y0_turned, XR * k + (s + 1 - XR))
                    sp.wait_ge(y0_stored[s], 16 * k)
                    sp.dma_start(ring[:, s, :], node_rows(x, XR * k + s)).then_inc(x0_loaded[s], 16)
            sp.wait_ge(y0_stored[0], 16 * X_ROUNDS)
            sp.wait_ge(y0_turned, TILES - XR)
            sp.dma_start(ring[0:LAST, 0, :], node_rows(x, TILES - 1)).then_inc(x0_loaded[0], 16)

            for layer in range(LAYERS - 1):
                def store(tile, layer=layer):
                    t, n, q, u = tile
                    sp.wait_ge(y_ready, n + 1)
                    sp.dma_start(node_rows(y_dram[layer + 1], t), y_sb[0:rows_of(t), q, :]).then_inc(y_stored[q], 16)

                run_layer(sp, layer, lambda i, first, tile: tile and store(tile), store)

            first_n = (LAYERS - 1) * TILES

            def load_x(tile):
                t, n, q, u = tile
                sp.dma_start(x_sb[0:rows_of(t), q, :], node_rows(x, t)).then_inc(x_loaded[q], 16)

            def finish(tile):
                t, n, q, u = tile
                sp.wait_ge(o_ready, n - first_n + 1)
                sp.dma_start(node_rows(out, t), y_sb[0:rows_of(t), q, :]).then_inc(o_stored[q], 16)

            def load_and_finish(i, first, tile):
                if tile:
                    load_x(tile)
                    finish(tile)

            run_layer(sp, LAYERS - 1, load_and_finish, lambda tile: load_and_finish(None, False, tile))
            for q in range(2):
                n = [k for k in range(first_n, first_n + TILES) if k % 2 == q]
                sp.wait_ge(o_stored[q], 16 * len(n))

        @block.gpsimd
        def _(pool):
            block6 = slice(FULL_BLOCKS * P, COLS)
            pool.memset(dst_rows[:, block6], N).then_inc(pads_ready, 1)
            pool.memset(src_rows[:, block6], 0).then_inc(pads_ready, 1)
            pool.memset(ones[:, :], 1.0).then_inc(consts_ready, 1)
            pool.memset(ident[:, :], 0.0).then_inc(consts_ready, 1)
            pool.wait_ge(consts_ready, 2)
            pool.affine_select(out=ident[:, :], in_=ident[:, :], compare_op=ALU.not_equal, fill=1.0, base=0,
                               pattern=[[-1, P]], channel_multiplier=1).then_inc(consts_ready, 1)
            pool.iota(win_iota[:, :], [[1, WIN]], base=0, channel_multiplier=0,
                      allow_small_or_imprecise_dtypes=True).then_inc(consts_ready, 1)
            pool.iota(lo_iota[:, :], [[1, P]], base=0, channel_multiplier=0,
                      allow_small_or_imprecise_dtypes=True).then_inc(consts_ready, 1)
            pool.iota(hi_iota[:, :], [[1, TILES]], base=0, channel_multiplier=0,
                      allow_small_or_imprecise_dtypes=True).then_inc(consts_ready, 1)

            pool.wait_ge(consts_ready, 6)
            pool.wait_ge(idx_done, 1)

            def hi_batch(j, buf, first):
                if not first:
                    pool.wait_ge(places_ready, j - 1)
                pool.tensor_tensor(hi_diff[:, buf, :, :],
                                   hi_iota[:, :].unsqueeze(1).broadcast_to([P, DEG_BATCH, TILES]),
                                   hi_f[:, bass.ds(DEG_BATCH * j, DEG_BATCH)].unsqueeze(2).broadcast_to([P, DEG_BATCH, TILES]),
                                   ALU.subtract).then_inc(hi_ready, 1)

            hi_batch(0, 0, True)
            hi_batch(1, 1, True)
            with pool.Fori(1, DEG_BATCHES // 2) as m:
                for r in range(2):
                    hi_batch(2 * m + r, r, False)

            for s in range(XR):
                pool.wait_ge(y0_stored[s], 16 * (X_ROUNDS + (s == 0)))
            for layer in range(LAYERS):

                def gather(i, first, tile, layer=layer):
                    for r in range(RING):
                        staged_count = pool.to_reg(layer * GROUPS + RING * i + (r + 1))
                        if layer == 0:
                            pool.wait_ge(y0_turned, TILES)
                        else:
                            for q in range(2):
                                pool.wait_ge(y_stored[q], 16 * ((layer * TILES + 1 - q) // 2))
                        pool.wait_ge(idx_staged, staged_count)
                        for k in range(CPG):
                            s = r * CPG + k
                            pool.indirect_dma_start(ring[:, s, :], None, y_dram[layer],
                                                    bass.IndirectOffsetOnAxis(ap=idx_stage[:, s:s + 1], axis=0),
                                                    bounds_check=N - 1, oob_is_err=False).then_inc(gathered[r], 16)

                run_layer(pool, layer, gather, lambda tile: None)

        @block.tensor
        def _(pe):
            pe.wait_ge(edges_turned_in, 2)
            pe.wait_ge(consts_ready, 6)
            for l, rows in enumerate((dst_rows_f, src_rows_f)):
                for b in range(ROW_BLOCKS):
                    mm = pe.transpose(ps[:, 2 * l + b // 4, (b % 4) * P:(b % 4 + 1) * P],
                                      rows[:, b * P:(b + 1) * P], ident[:, :])
                mm.then_inc(edges_turned, 1)
            pe.wait_ge(dst_ready, 1)
            pe.matmul(ps[:, 4, 0:GROUPS], ones[0:1, :], dst_f[0:1, 0:GROUPS * CPG:CPG],
                      start=True, stop=True).then_inc(base_spread, 1)

            pe.wait_ge(w_loaded, 16 * 6)
            at = [0]

            def weight_bank(needs):
                k = at[0]
                at[0] += 1
                if max(needs, k - 1) > 0:
                    pe.wait_ge(w_copied, max(needs, k - 1))
                return ps[:, 5 + k % 2, :]

            def turn_weight(w):
                for j in range(FB):
                    bank = weight_bank(0)
                    for i in range(FB):
                        mm = pe.transpose(bank[:, i * P:(i + 1) * P], w[:, i, j * P:(j + 1) * P], ident[:, :])
                    mm.then_inc(w_step, 1)

            def product(lhs, rhs, needs):
                bank = weight_bank(needs)
                for k in range(FB):
                    mm = pe.matmul(bank, lhs(k), rhs[:, k, :], start=(k == 0), stop=(k == FB - 1))
                mm.then_inc(w_step, 1)

            turn_weight(w2_sb)
            for i in range(FB):
                product(lambda k: wT[:, k, i * P:(i + 1) * P], w3_sb, FB)
            for l in range(2):
                bank = weight_bank(0)
                for k in range(FB):
                    mm = pe.matmul(bank[:, k * P:(k + 1) * P], b_row[0:1, l, k * P:(k + 1) * P], ones[0:1, :],
                                   start=True, stop=True)
                mm.then_inc(w_step, 1)
            for l, w in enumerate((w23, w3_sb)):
                product(lambda k: b_cols[:, l, k * P:(k + 1) * P], w, 2 * FB + 2)
            turn_weight(w1_sb)
            for i in range(FB):
                product(lambda k: wT[:, k, i * P:(i + 1) * P], w23, 3 * FB + 4)

            def deg_batch(j, buf, first, last):
                pe.wait_ge(places_ready, j + 1)
                for k in range(DEG_BATCH):
                    mm = pe.matmul(ps[:, 7, 0:TILES], lo_hot[:, buf, k, :], hi_hot[:, buf, k, :],
                                   start=(first and k == 0), stop=(last and k == DEG_BATCH - 1), skip_group_check=True)
                mm.then_inc(deg_counted, 1)

            deg_batch(0, 0, True, False)
            deg_batch(1, 1, False, False)
            with pe.Fori(1, DEG_BATCHES // 2 - 1) as m:
                for r in range(2):
                    deg_batch(2 * m + r, r, False, False)
            deg_batch(DEG_BATCHES - 2, 0, False, False)
            deg_batch(DEG_BATCHES - 1, 1, False, True)

            pe.wait_ge(w_copied, W_STEPS)

            def turn_y0(t, s, first):
                pe.wait_ge(y0_scaled, t + 1)
                if not first:
                    pe.wait_ge(acc_init, t - 1)
                for f in range(FB):
                    mm = pe.transpose(ps[:, 6 + s % 2, f * P:(f + 1) * P], ring[:, s, f * P:(f + 1) * P], ident[:, :])
                mm.then_inc(y0_turned, 1)

            for s in range(XR):
                turn_y0(s, s, s < 2)
            with pe.Fori(1, X_ROUNDS) as k:
                for s in range(XR):
                    turn_y0(XR * k + s, s, False)
            turn_y0(TILES - 1, 0, False)

            for layer in range(LAYERS):
                def sum_group(i, r, layer=layer):
                    pe.wait_ge(hot_ready, layer * GROUPS + RING * i + (r + 1))
                    pe.wait_ge(gathered[r], 16 * CPG * i + 16 * CPG * (layer * STEPS + 1))
                    for k in range(CPG):
                        for f in range(FB):
                            mm = pe.matmul(ps[:, r, f * WIN:(f + 1) * WIN], ring[:, r * CPG + k, f * P:(f + 1) * P],
                                           onehot[:, r, k, :], start=(k == 0 and f == 0),
                                           stop=(k == CPG - 1 and f == FB - 1), skip_group_check=True)
                    mm.then_inc(summed, 1)

                def turn_tile(tile, layer=layer):
                    t, n, q, u = tile
                    pe.wait_ge(tile_staged, n + 1)
                    if layer == LAYERS - 1 and not (isinstance(t, int) and t < 2):
                        pe.wait_ge(ln_step, LN_STEPS * (t - 2) + 1)
                    elif not (isinstance(n, int) and n < 2):
                        pe.wait_ge(h_ready, n - 1)
                    for k in range(FB):
                        if layer == 0:
                            mm = pe.matmul(ps[:, 4 + q, :], stage[:, q, k, :], w123[:, k, :],
                                           start=(k == 0), stop=(k == FB - 1))
                        else:
                            mm = pe.transpose(ps[:, 4 + q, k * P:(k + 1) * P], stage[:, q, k, :], ident[:, :])
                    mm.then_inc(tile_turned, 1)

                def turn_back(tile, layer=layer):
                    t, n, q, u = tile
                    pe.wait_ge(y_ready, n + 1)
                    pe.wait_ge(acc_init, n + (TILES - 1))
                    for f in range(FB):
                        mm = pe.transpose(ps[:, 6 + q, f * P:(f + 1) * P], y_sb[:, q, f * P:(f + 1) * P], ident[:, :])
                    mm.then_inc(y_turned, 1)

                def step(i, first, tile, layer=layer):
                    sum_group(i, 0)
                    sum_group(i, 1)
                    if tile:
                        turn_tile(tile)
                    sum_group(i, 2)
                    if tile and layer < LAYERS - 1:
                        turn_back(tile)
                    sum_group(i, 3)

                def tail(tile, layer=layer):
                    turn_tile(tile)
                    if layer < LAYERS - 1:
                        turn_back(tile)

                run_layer(pe, layer, step, tail)

        @block.scalar
        def _(act):
            dests = ([wT[:, k, :] for k in range(FB)] + [w23[:, k, :] for k in range(FB)]
                     + [b_cols[:, l, :] for l in range(2)] + [bias[:, l, :] for l in range(2)]
                     + [wT[:, k, :] for k in range(FB)] + [w123[:, k, :] for k in range(FB)])
            for k, d in enumerate(dests):
                act.wait_ge(w_step, k + 1)
                act.copy(d, ps[:, 5 + k % 2, :]).then_inc(w_copied, 1)

            act.wait_ge(deg_step, 1)
            act.activation(deg[:, 1, :], deg[:, 0, :], ACT.Sqrt).then_inc(sqrt_done, 1)

            def acc_tile(t):
                return acc[:, :, bass.ds(P * t, P)]

            def init_y0(t, s):
                act.wait_ge(y0_scaled, t + 1)
                act.dma_start(node_rows(y_dram[0], t), ring[0:rows_of(t), s, :]).then_inc(y0_stored[s], 16)
                act.wait_ge(y0_turned, t + 1)
                act.copy(acc_tile(t), ps[:, 6 + s % 2, :].rearrange("p (f n) -> p f n", n=P)).then_inc(acc_init, 1)

            with act.Fori(0, X_ROUNDS) as k:
                for s in range(XR):
                    init_y0(XR * k + s, s)
            init_y0(TILES - 1, 0)

            for layer in range(LAYERS):
                def stage_tile(tile, groups, layer=layer):
                    t, n, q, u = tile
                    act.wait_ge(added, layer * GROUPS + groups)
                    if not (isinstance(n, int) and n < 2):
                        act.wait_ge(tile_turned, n - 1)
                    act.copy(stage[:, q, :, :], acc_tile(t)).then_inc(tile_staged, 1)

                def scale_rows(tile):
                    t, n, q, u = tile
                    act.wait_ge(h_ready, n + 1)
                    if not (isinstance(n, int) and n < 2):
                        act.wait_ge(y_stored[q], 16 * u)
                        act.wait_ge(y_turned, n - 1)
                    act.activation(y_sb[:, q, :], h_sb[:, q, :], ACT.Copy, scale=dinv[:, bass.ds(t, 1)]).then_inc(y_ready, 1)

                def init_acc(tile, layer=layer):
                    t, n, q, u = tile
                    act.wait_ge(acc_init, TILES * (layer + 1))
                    act.wait_ge(y_turned, n + 1)
                    act.copy(acc_tile(t), ps[:, 6 + q, :].rearrange("p (f n) -> p f n", n=P)).then_inc(acc_init, 1)

                def std(tile, layer=layer):
                    t, n, q, u = tile
                    act.wait_ge(ln_step, LN_STEPS * (n - layer * TILES) + 5)
                    act.activation(ln[:, q, 9:10], ln[:, q, 8:9], ACT.Sqrt).then_inc(std_ready, 1)

                def work(tile, groups, layer=layer):
                    stage_tile(tile, groups)
                    if layer < LAYERS - 1:
                        scale_rows(tile)
                        init_acc(tile)
                    else:
                        std(tile)

                run_layer(act, layer, lambda i, first, tile: tile and work(tile, RING * i),
                          lambda tile: work(tile, GROUPS))

        @block.vector
        def _(dve):
            count = [0]

            def link(ins):
                count[0] += 1
                ins.then_inc(dve_done, 1)
                dve.wait_ge(dve_done, count[0])

            dve.wait_ge(edges_loaded, 16 * 6)
            dve.tensor_copy(dst_rows_f, dst_rows).then_inc(edges_turned_in, 1)
            dve.tensor_copy(src_rows_f, src_rows).then_inc(edges_turned_in, 1)
            dve.wait_ge(edges_turned, 1)
            turned = ps[:, :, :].rearrange("p b n -> p (b n)")
            link(dve.tensor_copy(dst_i, turned[:, 0:COLS]))
            dve.tensor_copy(dst_f, turned[:, 0:COLS]).then_inc(dst_ready, 1)
            link(dve.tensor_scalar(hi_i, dst_i, 7, None, ALU.arith_shift_right))
            link(dve.tensor_copy(hi_f, hi_i))
            link(dve.tensor_scalar(lo_i, dst_i, P - 1, None, ALU.bitwise_and))
            dve.tensor_copy(lo_f, lo_i).then_inc(idx_done, 1)
            dve.wait_ge(idx_done, 1)
            dve.wait_ge(edges_turned, 2)
            link(dve.tensor_copy(src_idx[:, :], turned[:, 1024:1024 + COLS]))
            dve.wait_ge(base_spread, 1)
            used = GROUPS * CPG
            link(dve.tensor_copy(base_i[:, :], ps[0:1, 4, 0:GROUPS]))
            dve.wait_ge(dst_ready, 1)
            link(dve.tensor_tensor(dst_rel[:, 0:used].rearrange("p (g k) -> p g k", k=CPG),
                                   dst_f[:, 0:used].rearrange("p (g k) -> p g k", k=CPG),
                                   ps[:, 4, 0:GROUPS].unsqueeze(2).broadcast_to([P, GROUPS, CPG]), ALU.subtract))

            dve.wait_ge(consts_ready, 6)

            def lo_batch(j, buf, first):
                if not first:
                    dve.wait_ge(deg_counted, j - 1)
                dve.wait_ge(hi_ready, j + 1)
                dve.tensor_scalar(hi_hot[:, buf, :, :], hi_diff[:, buf, :, :], 0.0, None, ALU.is_equal)
                for k in range(DEG_BATCH):
                    ins = dve.tensor_scalar(lo_hot[:, buf, k, :], lo_iota[:, :], lo_f[:, bass.ds(DEG_BATCH * j + k, 1)],
                                            None, ALU.is_equal)
                ins.then_inc(places_ready, 1)

            lo_batch(0, 0, True)
            lo_batch(1, 1, True)
            with dve.Fori(1, DEG_BATCHES // 2) as m:
                for r in range(2):
                    lo_batch(2 * m + r, r, False)

            dve.wait_ge(deg_counted, DEG_BATCHES)
            d, root, t1 = deg[:, 0, :], deg[:, 1, :], deg[:, 2, :]
            dve.tensor_scalar(d, ps[:, 7, 0:TILES], 1.0, None, ALU.add).then_inc(deg_step, 1)
            dve.wait_ge(sqrt_done, 1)
            link(dve.reciprocal(root, root))
            link(dve.tensor_tensor(t1, root, root, ALU.mult))
            link(dve.tensor_tensor(t1, t1, d, ALU.mult))
            link(dve.tensor_scalar(t1, t1, -0.5, 1.5, ALU.mult, ALU.add))
            dve.tensor_tensor(dinv[:, :], root, t1, ALU.mult).then_inc(dinv_ready, 1)
            dve.wait_ge(dinv_ready, 1)
            link(dve.memset(acc[:, :, TILES * P:ACC_W], 0.0))

            def scale_y0(t, s, k):
                dve.wait_ge(x0_loaded[s], 16 * k + 16)
                dve.tensor_scalar(ring[:, s, :], ring[:, s, :], dinv[:, bass.ds(t, 1)], None, ALU.mult).then_inc(y0_scaled, 1)

            with dve.Fori(0, X_ROUNDS) as k:
                for s in range(XR):
                    scale_y0(XR * k + s, s, k)
            scale_y0(TILES - 1, 0, X_ROUNDS)

            def stage_group(g, r):
                cols = bass.ds(CPG * g, CPG)
                dve.tensor_copy(idx_stage[:, r * CPG:(r + 1) * CPG], src_idx[:, cols]).then_inc(idx_staged, 1)
                dve.tensor_tensor(onehot[:, r, :, :], win_iota[:, :].unsqueeze(1).broadcast_to([P, CPG, WIN]),
                                  dst_rel[:, cols].unsqueeze(2).broadcast_to([P, CPG, WIN]),
                                  ALU.is_equal).then_inc(hot_ready, 1)

            for r in range(RING):
                stage_group(r, r)
            for layer in range(LAYERS):
                dve.wait_ge(acc_init, TILES * (layer + 1))

                def add_group(i, r, first, layer=layer):
                    g = RING * i + r
                    dve.wait_ge(summed, layer * GROUPS + g + 1)
                    if not (first and r == 0 and layer == 0):
                        dve.wait_ge(added, layer * GROUPS + g)
                    base = dve.value_load(base_i[0:1, bass.ds(g, 1)], min_val=0, max_val=N)
                    window = acc[:, :, bass.ds(base, WIN)]
                    dve.tensor_tensor(window, window, ps[:, r, 0:FB * WIN].rearrange("p (f w) -> p f w", w=WIN),
                                      ALU.add).then_inc(added, 1)
                    if not (isinstance(i, int) and i == STEPS - 1):
                        stage_group(g + RING, r)
                    elif layer < LAYERS - 1:
                        stage_group(r, r)

                def bias_rows(tile, layer=layer):
                    t, n, q, u = tile
                    dve.wait_ge(tile_turned, n + 1)
                    if not (isinstance(n, int) and n < 2):
                        dve.wait_ge(y_ready, n - 1)
                    dve.scalar_tensor_tensor(out=h_sb[:, q, :], in0=ps[:, 4 + q, :], scalar=dinv[:, bass.ds(t, 1)],
                                             in1=bias[:, layer, :], op0=ALU.mult, op1=ALU.add).then_inc(h_ready, 1)

                def norm_rows(tile, layer=layer):
                    t, n, q, u = tile
                    n_here = n - layer * TILES
                    row = h_sb[:, q, :]
                    done = LN_STEPS * n_here
                    dve.wait_ge(tile_turned, n + 1)
                    dve.wait_ge(x_loaded[q], 16 * (u - (layer * TILES + 1 - q) // 2 + 1))
                    dve.scalar_tensor_tensor(out=row, in0=ps[:, 4 + q, :], scalar=dinv[:, bass.ds(t, 1)],
                                             in1=x_sb[:, q, :], op0=ALU.mult, op1=ALU.add).then_inc(ln_step, 1)
                    dve.wait_ge(ln_step, done + 1)
                    dve.tensor_tensor(row, row, bias[:, layer, :], ALU.add).then_inc(ln_step, 1)
                    dve.wait_ge(ln_step, done + 2)
                    dve.bn_stats(ln[:, q, 0:6], row).then_inc(ln_step, 1)
                    stats_done = dve.to_reg(done + 3)
                    dve.wait_ge(w_loaded, 16 * 6)
                    dve.wait_ge(ln_step, stats_done)
                    dve.bn_aggr(ln[:, q, 6:8], ln[:, q, 0:6]).then_inc(ln_step, 1)
                    dve.wait_ge(ln_step, done + 4)
                    dve.tensor_scalar(ln[:, q, 8:9], ln[:, q, 7:8], EPS, None, ALU.add).then_inc(ln_step, 1)
                    dve.wait_ge(std_ready, n_here + 1)
                    dve.reciprocal(ln[:, q, 10:11], ln[:, q, 9:10]).then_inc(ln_step, 1)
                    dve.wait_ge(ln_step, done + 6)
                    before = (layer * TILES + 1 - q) // 2
                    if isinstance(n_here, int) and n_here < 2:
                        dve.wait_ge(y_stored[q], 16 * before)
                        dve.wait_ge(y_turned, layer * TILES)
                    else:
                        dve.wait_ge(o_stored[q], 16 * (u - before))
                    dve.tensor_scalar(y_sb[:, q, :], row, ln[:, q, 6:7], ln[:, q, 10:11],
                                      ALU.subtract, ALU.mult).then_inc(o_ready, 1)

                rows = bias_rows if layer < LAYERS - 1 else norm_rows

                def step(i, first, tile, layer=layer):
                    add_group(i, 0, first)
                    add_group(i, 1, first)
                    if tile:
                        rows(tile)
                    add_group(i, 2, first)
                    add_group(i, 3, first)

                run_layer(dve, layer, step, rows)


_INS = ["x", "src", "dst", "L0_gnn_W1", "L0_gnn_b1", "L0_gnn_W2", "L0_gnn_b2", "L0_gnn_W3", "L0_gnn_b3"]


def kernel(**inputs):
    import concourse.bacc as bacc
    import numpy as np
    from concourse.bass_utils import run_bass_kernel_spmd

    nc = bacc.Bacc("TRN2", target_bir_lowering=False, num_devices=1)
    arrays, aps = {}, []
    for name in _INS:
        a = np.ascontiguousarray(inputs[name])
        arrays[f"in_{name}_dram"] = a
        aps.append(nc.dram_tensor(f"in_{name}_dram", a.shape, mybir.dt.from_np(a.dtype), kind="ExternalInput").ap())
    out = nc.dram_tensor("out_0_dram", inputs["x"].shape, F32, kind="ExternalOutput").ap()
    gcn_three_layers_resnorm(nc, *aps, out)
    result = run_bass_kernel_spmd(nc, [arrays], core_ids=[0])
    return result.results[0]["out_0_dram"]
```

```python
from contextlib import ExitStack

import concourse.bass as bass
from concourse import mybir

F32 = mybir.dt.float32
I32 = mybir.dt.int32
BF16 = mybir.dt.bfloat16
ALU = mybir.AluOpType
ACT = mybir.ActivationFunctionType
AX = mybir.AxisListType

P = 128
EPS = 1e-5
LAYERS = 3
CPQ = 4
QUADS = 4
CPS = CPQ * QUADS
GPS = 2
LAG = 5
POOL_LO = 3


def gcn_three_layers_resnorm(nc, x, src, dst, W1, b1, W2, b2, W3, b3, out):
    N, D = x.shape
    E = src.shape[0]
    FB = D // P
    TILES = -(-N // P)
    LAST = N - (TILES - 1) * P
    STEPS = -(-E // (P * CPS))
    GROUPS = STEPS * GPS
    CHUNKS = STEPS * CPS
    ROW_BLOCKS = -(-CHUNKS // P)
    COLS = ROW_BLOCKS * P
    FULL_ROWS = E // P
    FULL_BLOCKS = FULL_ROWS // P
    TAIL_ROWS = FULL_ROWS - FULL_BLOCKS * P
    TAIL_EDGES = E - FULL_ROWS * P
    X_BATCH = 4
    X_BATCHES = (TILES - 1) // X_BATCH
    LN_STEPS = 6
    W_STEPS = 4 * FB + 4
    assert D == 512 and STEPS % 2 == 0 and LAG + 1 < STEPS and LAST < P and TAIL_EDGES
    assert (TILES - 1) % X_BATCH == 0 and STEPS - LAG <= TILES and FULL_BLOCKS + 1 == ROW_BLOCKS

    y_dram = [nc.dram_tensor(f"y{l}_dram", [N, D], F32, kind="Internal").ap() for l in range(LAYERS)]

    with ExitStack() as ctx:
        def sb(name, shape, dt):
            return ctx.enter_context(nc.sbuf_tensor(name, shape, dt))

        def sem(name):
            return ctx.enter_context(nc.semaphore(name))

        acc = sb("acc", [P, (TILES + 1) * D], F32)
        ring = sb("ring", [P, CPS, D], F32)
        onehot = sb("onehot", [P, QUADS, CPQ, P], F32)
        src_idx = sb("src_idx", [P, COLS], I32)
        lo_f = sb("lo_f", [P, COLS], F32)
        idx_stage = sb("idx_stage", [P, CPS], I32)
        mask = sb("mask", [P, 2, GROUPS], F32)
        group_tile = sb("group_tile", [1, GROUPS], I32)
        w123 = sb("w123", [P, FB, D], F32)
        w1_sb = sb("w1_sb", [P, FB, D], F32)
        w2_sb = sb("w2_sb", [P, FB, D], F32)
        w23 = sb("w23", [P, FB, D], F32)
        wT = sb("wT", [P, FB, D], F32)
        bias = sb("bias", [P, LAYERS, D], F32)
        row_sb = sb("row_sb", [P, D], F32)
        h_sb = sb("h_sb", [P, D], F32)
        ident = sb("ident", [P, P], F32)
        ones = sb("ones", [P, P], F32)
        place_iota = sb("place_iota", [P, P], F32)
        tile_iota = sb("tile_iota", [P, TILES], F32)
        own_place = sb("own_place", [P, 1], F32)
        step_first = sb("step_first", [P, STEPS], F32)
        tile_first = sb("tile_first", [P, TILES], F32)
        broken = sb("broken", [P, 4], F32)
        unordered = sb("unordered", [1, 1], I32)
        dinv = sb("dinv", [P, TILES], F32)
        deg = sb("deg", [P, 3, TILES], F32)
        ln = sb("ln", [P, 12], F32)

        w3_sb = w123
        x_sb = w1_sb[:, 0, :]
        turned_sb = w2_sb[:, 0, :]
        tmp = ring[:, :, :].rearrange("p c d -> p (c d)")
        cut = [0]

        def carve(words):
            cut[0] += words
            return tmp[:, cut[0] - words:cut[0]]

        def places(chunks, width):
            return carve(2 * chunks * width // 2).bitcast(BF16).rearrange("p (b c n) -> p b c n", b=2, c=chunks)

        src_rows = carve(COLS)
        dst_rows = carve(COLS)
        dst_f = carve(COLS)
        dst_i = carve(COLS).bitcast(I32)
        hi_i = carve(COLS).bitcast(I32)
        hi_f = hi_i.bitcast(F32)
        lo_hot = places(CPS, P)
        hi_hot = places(CPS, TILES)
        hi_diff = places(CPS, TILES)
        lo_diff = h_sb[:, 0:POOL_LO * P].bitcast(BF16).rearrange("p (b c n) -> p b c n", b=2, c=POOL_LO)
        assert cut[0] <= CPS * D
        small = onehot[:, :, :, :].rearrange("p q c n -> p (q c n)")
        b_row = small[:, 0:2 * D].rearrange("p (l d) -> p l d", l=2)
        b_cols = small[:, 2 * D:4 * D].rearrange("p (l d) -> p l d", l=2)
        order_gap = wT[:, 0:2, :].rearrange("p k n -> p (k n)")[:, 0:CHUNKS]
        group_base = w23[:, 0, 0:GROUPS]
        group_int = w23[:, 1, 0:GROUPS].bitcast(I32)
        group_place = w23[:, 2, 0:GROUPS]

        dst_keep = wT[:, 2:4, :].rearrange("p k n -> p (k n)")[:, 0:CHUNKS]
        dst_off = w23[:, 3, 0:CPS]

        ps = ctx.enter_context(nc.psum_tensor("ps", [P, 8, 512], F32))
        ORDER_BANK, TURN_BANK, PRODUCT_BANK, DEG_BANK = 3, 4, 5, 7

        consts_ready = sem("consts_ready")
        pads_ready = sem("pads_ready")
        tail_zeroed = sem("tail_zeroed")
        dst_loaded = sem("dst_loaded")
        src_loaded = sem("src_loaded")
        w_loaded = sem("w_loaded")
        x_all_loaded = sem("x_all_loaded")
        dve_done = sem("dve_done")
        rows_float = sem("rows_float")
        edges_turned = sem("edges_turned")
        dst_ready = sem("dst_ready")
        places_known = sem("places_known")
        base_spread = sem("base_spread")
        diff_ready = sem("diff_ready")
        places_ready = sem("places_ready")
        deg_counted = sem("deg_counted")
        deg_ready = sem("deg_ready")
        sqrt_done = sem("sqrt_done")
        dinv_ready = sem("dinv_ready")
        w_step = sem("w_step")
        w_copied = sem("w_copied")
        y0_scaled = sem("y0_scaled")
        y0_stored = sem("y0_stored")
        groups_ready = sem("groups_ready")
        order_checked = sem("order_checked")
        order_summed = sem("order_summed")
        path_known = sem("path_known")
        idx_staged = sem("idx_staged")
        hot_ready = sem("hot_ready")
        gathered = [sem(f"gathered{r}") for r in range(QUADS)]
        summed = sem("summed")
        added = sem("added")
        tile_staged = sem("tile_staged")
        tile_turned = sem("tile_turned")
        turn_copied = sem("turn_copied")
        tile_multiplied = sem("tile_multiplied")
        h_ready = sem("h_ready")
        y_ready = sem("y_ready")
        y_stored = sem("y_stored")
        x_loaded = sem("x_loaded")
        ln_step = sem("ln_step")
        std_ready = sem("std_ready")
        o_ready = sem("o_ready")
        o_stored = sem("o_stored")

        any_staged = sem("any_staged")
        any_gathered = sem("any_gathered")
        any_off = sem("any_off")
        any_hot = sem("any_hot")
        any_summed = sem("any_summed")
        any_added = sem("any_added")

        block = ctx.enter_context(nc.Block())

        def run_layer(eng, step, tail):
            step(0, None)
            with eng.Fori(1, LAG) as i:
                step(i, None)
            step(LAG, 0)
            with eng.Fori(LAG + 1, STEPS - 1) as i:
                step(i, i - LAG)
            step(STEPS - 1, STEPS - 1 - LAG)
            for t in range(STEPS - LAG, TILES):
                tail(t)

        def run_tiles(eng, work):
            work(0)
            with eng.Fori(1, TILES - 1) as t:
                work(t)
            work(TILES - 1)

        def order_holds(eng):
            eng.wait_ge(path_known, 1)
            return eng.If_eq(eng.to_reg(eng.value_load(unordered[0:1, 0:1])), 0)

        def fast_done(layer, i):
            return 2 * GPS * i + 2 * layer * GROUPS

        def any_done(layer):
            return (layer + 1) * STEPS * TILES + 1

        def is_static(v, value):
            return isinstance(v, int) and v == value

        def rows_of(t):
            return LAST if is_static(t, TILES - 1) else P

        def node_rows(dram, t):
            return dram[bass.ds(P * t, rows_of(t)), :]

        def tile_of(t):
            return acc[:, bass.ds(D * t, D)]

        @block.sync
        def _(sp):
            tail_at = FULL_BLOCKS * P * P
            lists = ((dst_rows.bitcast(I32).rearrange("c (b p) -> c b p", p=P), dst, dst_loaded),
                     (src_rows.bitcast(I32).rearrange("c (b p) -> c b p", p=P), src, src_loaded))
            sp.wait_ge(pads_ready, 2)
            for r3, edges, loaded in lists:
                sp.dma_start(r3[:, 0:FULL_BLOCKS, :],
                             edges[0:tail_at].rearrange("(b c p) -> c b p", c=P, p=P)).then_inc(loaded, 16)
                sp.dma_start(r3[0:TAIL_ROWS, FULL_BLOCKS, :],
                             edges[tail_at:tail_at + TAIL_ROWS * P].rearrange("(c p) -> c p", p=P)).then_inc(loaded, 16)
                sp.dma_start(r3[TAIL_ROWS:TAIL_ROWS + 1, FULL_BLOCKS, 0:TAIL_EDGES],
                             edges[tail_at + TAIL_ROWS * P:E].rearrange("(c p) -> c p", c=1)).then_inc(loaded, 16)
            for t, w in ((w2_sb, W2), (w3_sb, W3), (w1_sb, W1)):
                sp.dma_start(t[:, :, :], w.rearrange("(k p) n -> p k n", p=P)).then_inc(w_loaded, 16)
            for l, b in enumerate((b1, b2)):
                sp.dma_start(b_row[0:1, l, :], b.rearrange("(a d) -> a d", a=1)).then_inc(w_loaded, 16)
            sp.dma_start(bias[:, 2, :], b3.rearrange("(a d) -> a d", a=1).broadcast_to([P, D])).then_inc(w_loaded, 16)

            whole = (TILES - 1) * P
            sp.dma_start(acc[:, 0:(TILES - 1) * D].rearrange("p (t d) -> p t d", d=D),
                         x[0:whole, :].rearrange("(t p) d -> p t d", p=P)).then_inc(x_all_loaded, 16)
            sp.wait_ge(tail_zeroed, 1)
            sp.dma_start(acc[0:LAST, (TILES - 1) * D:TILES * D], x[whole:N, :]).then_inc(x_all_loaded, 16)

            with sp.Fori(0, X_BATCHES) as k:
                sp.wait_ge(y0_scaled, X_BATCH * k + X_BATCH)
                sp.dma_start(y_dram[0][bass.ds(X_BATCH * P * k, X_BATCH * P), :].rearrange("(t p) d -> p t d", p=P),
                             acc[:, bass.ds(X_BATCH * D * k, X_BATCH * D)].rearrange("p (t d) -> p t d", d=D)
                             ).then_inc(y0_stored, 16)
            sp.wait_ge(y0_scaled, TILES)
            sp.dma_start(node_rows(y_dram[0], TILES - 1), acc[0:LAST, (TILES - 1) * D:TILES * D]).then_inc(y0_stored, 16)

            def store(layer, t):
                sp.wait_ge(y_ready, layer * TILES + t + 1)
                sp.dma_start(node_rows(y_dram[layer + 1], t), acc[0:rows_of(t), bass.ds(D * t, D)]).then_inc(y_stored, 16)

            def load_and_finish(t):
                if not is_static(t, 0):
                    sp.wait_ge(ln_step, LN_STEPS * t + (1 - LN_STEPS))
                sp.dma_start(x_sb[0:rows_of(t), :], node_rows(x, t)).then_inc(x_loaded, 16)
                sp.wait_ge(o_ready, t + 1)
                sp.dma_start(node_rows(out, t), row_sb[0:rows_of(t), :]).then_inc(o_stored, 16)

            def tile_work(layer, t):
                if t is not None:
                    if layer < LAYERS - 1:
                        store(layer, t)
                    else:
                        load_and_finish(t)

            with order_holds(sp):
                for layer in range(LAYERS):
                    run_layer(sp, lambda i, t: tile_work(layer, t), lambda t: tile_work(layer, t))
            with sp.Else():
                for layer in range(LAYERS):
                    run_tiles(sp, lambda t: tile_work(layer, t))
            sp.wait_ge(o_stored, 16 * TILES)

        @block.gpsimd
        def _(pool):
            pads = slice(FULL_BLOCKS * P, COLS)
            pool.memset(dst_rows[:, pads].bitcast(I32), N).then_inc(pads_ready, 1)
            pool.memset(src_rows[:, pads].bitcast(I32), 0).then_inc(pads_ready, 1)
            pool.memset(ident[:, :], 0.0).then_inc(consts_ready, 1)
            pool.memset(ones[:, :], 1.0).then_inc(consts_ready, 1)
            pool.wait_ge(consts_ready, 2)
            pool.affine_select(out=ident[:, :], in_=ident[:, :], compare_op=ALU.not_equal, fill=1.0, base=0,
                               pattern=[[-1, P]], channel_multiplier=1).then_inc(consts_ready, 1)
            for row, by, width, base, down in ((place_iota, 1, P, 0, 0), (tile_iota, 1, TILES, 0, 0), (own_place, 1, 1, 0, 1),
                                               (tile_first, P, TILES, 0, 0), (step_first, P, STEPS, P * (1 - LAG), 0)):
                pool.iota(row[:, :], [[by, width]], base=base, channel_multiplier=down,
                          allow_small_or_imprecise_dtypes=True).then_inc(consts_ready, 1)
            pool.memset(acc[:, (TILES - 1) * D:], 0.0).then_inc(tail_zeroed, 1)

            pool.wait_ge(consts_ready, 8)
            pool.wait_ge(places_known, 2)

            def difference(out_, iota, edge, j, chunks, width):
                return pool.tensor_tensor(out_, iota[:, :].unsqueeze(1).broadcast_to([P, chunks, width]),
                                          edge[:, bass.ds(CPS * j, chunks)].unsqueeze(2).broadcast_to([P, chunks, width]),
                                          ALU.subtract)

            def diff_batch(j, buf, first):
                if not first:
                    pool.wait_ge(places_ready, j - 1)
                difference(lo_diff[:, buf, :, :], place_iota, lo_f, j, POOL_LO, P).then_inc(diff_ready, 1)
                difference(hi_diff[:, buf, :, :], tile_iota, hi_f, j, CPS, TILES).then_inc(diff_ready, 1)

            diff_batch(0, 0, True)
            diff_batch(1, 1, True)
            with pool.Fori(1, STEPS // 2) as m:
                for buf in range(2):
                    diff_batch(2 * m + buf, buf, False)

            def rows_stored(layer):
                if layer == 0:
                    pool.wait_ge(y0_stored, 16 * (X_BATCHES + 1))
                else:
                    pool.wait_ge(y_stored, 16 * TILES * layer)

            def gather(layer, s, landed):
                pool.indirect_dma_start(ring[:, s, :], None, y_dram[layer],
                                        bass.IndirectOffsetOnAxis(ap=idx_stage[:, s:s + 1], axis=0),
                                        bounds_check=N - 1, oob_is_err=False).then_inc(landed, 16)

            def gather_step(layer, i):
                for r in range(QUADS):
                    quad = pool.to_reg(layer * STEPS * QUADS + QUADS * i + (r + 1))
                    rows_stored(layer)
                    pool.wait_ge(idx_staged, quad)
                    for k in range(CPQ):
                        gather(layer, r * CPQ + k, gathered[r])

            def gather_any(layer, i):
                turn = pool.to_reg(layer * STEPS + 1 + i)
                rows_stored(layer)
                pool.wait_ge(any_staged, turn)
                for s in range(CPS):
                    gather(layer, s, any_gathered)

            with order_holds(pool):
                for layer in range(LAYERS):
                    run_layer(pool, lambda i, t: gather_step(layer, i), lambda t: None)
            with pool.Else():
                for layer in range(LAYERS):
                    with pool.Fori(0, STEPS) as i:
                        gather_any(layer, i)

        @block.tensor
        def _(pe):
            pe.wait_ge(consts_ready, 8)
            for l, rows in enumerate((dst_rows, src_rows)):
                pe.wait_ge(rows_float, l + 1)
                for b in range(ROW_BLOCKS):
                    mm = pe.transpose(ps[:, 2 * l + b // 4, (b % 4) * P:(b % 4 + 1) * P],
                                      rows[:, b * P:(b + 1) * P], ident[:, :])
                mm.then_inc(edges_turned, 1)
            pe.wait_ge(dst_ready, 1)
            pe.matmul(ps[:, 4, 0:GROUPS], ones[0:1, :], dst_f[0:1, 0:CHUNKS:CPS // GPS],
                      start=True, stop=True).then_inc(base_spread, 1)

            def deg_batch(j, buf, first, last):
                pe.wait_ge(places_ready, j + 1)
                for k in range(CPS):
                    mm = pe.matmul(ps[:, DEG_BANK, 0:TILES], lo_hot[:, buf, k, :], hi_hot[:, buf, k, :],
                                   start=(first and k == 0), stop=(last and k == CPS - 1), skip_group_check=True)
                mm.then_inc(deg_counted, 1)

            def deg_pairs(a, b):
                with pe.Fori(a, b) as m:
                    for buf in range(2):
                        deg_batch(2 * m + buf, buf, False, False)

            at = [0]

            def weight_bank(needs):
                k = at[0]
                at[0] += 1
                if max(needs, k - 1) > 0:
                    pe.wait_ge(w_copied, max(needs, k - 1))
                return ps[:, 5 + k % 2, :]

            def turn_weight(w, j):
                bank = weight_bank(0)
                for i in range(FB):
                    mm = pe.transpose(bank[:, i * P:(i + 1) * P], w[:, i, j * P:(j + 1) * P], ident[:, :])
                mm.then_inc(w_step, 1)

            def product(lhs, rhs, needs):
                bank = weight_bank(needs)
                for k in range(FB):
                    mm = pe.matmul(bank, lhs(k), rhs[:, k, :], start=(k == 0), stop=(k == FB - 1))
                mm.then_inc(w_step, 1)

            def spread_bias(l):
                bank = weight_bank(0)
                for k in range(FB):
                    mm = pe.matmul(bank[:, k * P:(k + 1) * P], b_row[0:1, l, k * P:(k + 1) * P], ones[0:1, :],
                                   start=True, stop=True)
                mm.then_inc(w_step, 1)

            def weight_step(k):
                if k < FB:
                    turn_weight(w2_sb, k)
                elif k < 2 * FB:
                    product(lambda j: wT[:, j, (k - FB) * P:(k - FB + 1) * P], w3_sb, FB)
                elif k < 2 * FB + 2:
                    spread_bias(k - 2 * FB)
                elif k < 2 * FB + 4:
                    l = k - 2 * FB - 2
                    product(lambda j: b_cols[:, l, j * P:(j + 1) * P], (w23, w3_sb)[l], 2 * FB + 2)
                elif k < 3 * FB + 4:
                    turn_weight(w1_sb, k - 2 * FB - 4)
                else:
                    i = k - 3 * FB - 4
                    product(lambda j: wT[:, j, i * P:(i + 1) * P], w23, 3 * FB + 4)

            deg_batch(0, 0, True, False)
            deg_batch(1, 1, False, False)
            pe.wait_ge(w_loaded, 16 * 6)
            pairs = STEPS // 2 - 1
            for k in range(W_STEPS // 2):
                weight_step(2 * k)
                weight_step(2 * k + 1)
                deg_pairs(1 + (pairs - 1) * k // (W_STEPS // 2), 1 + (pairs - 1) * (k + 1) // (W_STEPS // 2))
            deg_batch(STEPS - 2, 0, False, False)
            deg_batch(STEPS - 1, 1, False, True)

            pe.wait_ge(order_checked, 1)
            pe.matmul(ps[0:1, ORDER_BANK, 0:1], broken[:, 0:1], ones[:, 0:1], start=True, stop=True).then_inc(order_summed, 1)

            def sum_quad(layer, i, r):
                bank = r * GPS // QUADS
                pe.wait_ge(hot_ready, layer * STEPS * QUADS + QUADS * i + (r + 1))
                pe.wait_ge(gathered[r], 16 * CPQ * i + 16 * CPQ * (layer * STEPS + 1))
                opens, closes = r % GPS == 0, r % GPS == GPS - 1
                if opens and not (layer == 0 and is_static(i, 0)):
                    pe.wait_ge(added, 2 * GPS * i + 2 * (layer * GROUPS + bank + 1 - GPS))
                for k in range(CPQ):
                    mm = pe.matmul(ps[:, bank, :], onehot[:, r, k, :], ring[:, r * CPQ + k, :],
                                   start=(opens and k == 0), stop=(closes and k == CPQ - 1), skip_group_check=True)
                mm.then_inc(summed, 1)

            def turn_tile(t):
                pe.wait_ge(tile_staged, t + 1)
                if not is_static(t, 0):
                    pe.wait_ge(turn_copied, t)
                for k in range(FB):
                    mm = pe.transpose(ps[:, TURN_BANK, k * P:(k + 1) * P], row_sb[:, k * P:(k + 1) * P], ident[:, :])
                mm.then_inc(tile_turned, 1)

            def multiply_tile(t):
                pe.wait_ge(turn_copied, t + 1)
                if not is_static(t, 0):
                    pe.wait_ge(h_ready, t)
                for k in range(FB):
                    mm = pe.matmul(ps[:, PRODUCT_BANK, :], turned_sb[:, k * P:(k + 1) * P], w123[:, k, :],
                                   start=(k == 0), stop=(k == FB - 1))
                mm.then_inc(tile_multiplied, 1)

            def step(layer, i, t):
                sum_quad(layer, i, 0)
                sum_quad(layer, i, 1)
                if layer == 0 and t is not None:
                    turn_tile(t)
                sum_quad(layer, i, 2)
                if layer == 0 and t is not None:
                    multiply_tile(t)
                sum_quad(layer, i, 3)

            def tail(layer, t):
                if layer == 0:
                    turn_tile(t)
                    multiply_tile(t)

            def sum_any(layer, i, t):
                pe.wait_ge(any_gathered, 16 * CPS * i + 16 * CPS * (layer * STEPS + 1))
                pe.wait_ge(any_hot, TILES * i + t + (layer * STEPS * TILES + 1))
                for s in range(CPS):
                    mm = pe.matmul(ps[:, 0, :], onehot[:, s // CPQ, s % CPQ, :], ring[:, s, :],
                                   start=(s == 0), stop=(s == CPS - 1))
                mm.then_inc(any_summed, 1)

            with order_holds(pe):
                for layer in range(LAYERS):
                    run_layer(pe, lambda i, t: step(layer, i, t), lambda t: tail(layer, t))
            with pe.Else():
                for layer in range(LAYERS):
                    with pe.Fori(0, STEPS) as i:
                        with pe.Fori(0, TILES) as t:
                            sum_any(layer, i, t)
                    if layer == 0:
                        run_tiles(pe, lambda t: tail(0, t))

        @block.scalar
        def _(act):
            dests = ([wT[:, k, :] for k in range(FB)] + [w23[:, k, :] for k in range(FB)]
                     + [b_cols[:, l, :] for l in range(2)] + [bias[:, l, :] for l in range(2)]
                     + [wT[:, k, :] for k in range(FB)] + [w123[:, k, :] for k in range(FB)])
            for k, d in enumerate(dests):
                act.wait_ge(w_step, k + 1)
                act.copy(d, ps[:, 5 + k % 2, :]).then_inc(w_copied, 1)

            act.wait_ge(deg_ready, 1)
            act.activation(deg[:, 1, :], deg[:, 0, :], ACT.Sqrt).then_inc(sqrt_done, 1)

            act.wait_ge(dinv_ready, 1)
            act.wait_ge(x_all_loaded, 32)
            with act.Fori(0, X_BATCHES) as k:
                for r in range(X_BATCH):
                    t = X_BATCH * k + r
                    act.activation(tile_of(t), tile_of(t), ACT.Copy, scale=dinv[:, bass.ds(t, 1)]).then_inc(y0_scaled, 1)
            act.activation(tile_of(TILES - 1), tile_of(TILES - 1), ACT.Copy,
                           scale=dinv[:, TILES - 1:TILES]).then_inc(y0_scaled, 1)

            def turn_rows(t):
                if not is_static(t, 0):
                    act.wait_ge(tile_turned, t)
                act.activation(row_sb[:, :], tile_of(t), ACT.Copy).then_inc(tile_staged, 1)
                act.wait_ge(tile_turned, t + 1)
                if not is_static(t, 0):
                    act.wait_ge(tile_multiplied, t)
                act.activation(turned_sb, ps[:, TURN_BANK, :], ACT.Copy).then_inc(turn_copied, 1)

            def scale_rows(layer, t):
                act.wait_ge(h_ready, layer * TILES + t + 1)
                act.activation(tile_of(t), h_sb[:, :], ACT.Copy, scale=dinv[:, bass.ds(t, 1)]).then_inc(y_ready, 1)

            def std(t):
                act.wait_ge(ln_step, LN_STEPS * t + 5)
                act.activation(ln[:, 9:10], ln[:, 8:9], ACT.Sqrt).then_inc(std_ready, 1)

            def work(layer, t, sums, count):
                if t is None:
                    return
                if layer == 0:
                    act.wait_ge(sums, count)
                    turn_rows(t)
                if layer < LAYERS - 1:
                    scale_rows(layer, t)
                else:
                    std(t)

            with order_holds(act):
                for layer in range(LAYERS):
                    run_layer(act, lambda i, t: work(layer, t, added, fast_done(layer, i)),
                              lambda t: work(layer, t, added, fast_done(layer, STEPS)))
            with act.Else():
                for layer in range(LAYERS):
                    run_tiles(act, lambda t: work(layer, t, any_added, any_done(layer)))

        @block.vector
        def _(dve):
            count = [0]

            def link(ins):
                count[0] += 1
                ins.then_inc(dve_done, 1)
                dve.wait_ge(dve_done, count[0])

            turned = ps[:, :, :].rearrange("p b n -> p (b n)")
            dve.wait_ge(dst_loaded, 16 * 3)
            dve.tensor_copy(dst_rows, dst_rows.bitcast(I32)).then_inc(rows_float, 1)
            dve.wait_ge(src_loaded, 16 * 3)
            dve.tensor_copy(src_rows, src_rows.bitcast(I32)).then_inc(rows_float, 1)
            dve.wait_ge(edges_turned, 1)
            link(dve.tensor_copy(dst_i, turned[:, 0:COLS]))
            link(dve.tensor_scalar(hi_i, dst_i, 7, None, ALU.arith_shift_right))
            dve.tensor_copy(hi_f, hi_i).then_inc(places_known, 1)
            link(dve.tensor_scalar(dst_i, dst_i, P - 1, None, ALU.bitwise_and))
            dve.tensor_copy(lo_f[:, :], dst_i).then_inc(places_known, 1)
            dve.tensor_copy(dst_f, turned[:, 0:COLS]).then_inc(dst_ready, 1)
            dve.wait_ge(edges_turned, 2)
            dve.tensor_copy(src_idx[:, :], turned[:, 1024:1024 + COLS])

            dve.wait_ge(consts_ready, 8)
            dve.wait_ge(places_known, 2)

            def place_batch(j, buf, first):
                if not first:
                    dve.wait_ge(deg_counted, j - 1)
                chunks = CPS - POOL_LO
                dve.tensor_tensor(lo_hot[:, buf, POOL_LO:, :], place_iota[:, :].unsqueeze(1).broadcast_to([P, chunks, P]),
                                  lo_f[:, bass.ds(CPS * j + POOL_LO, chunks)].unsqueeze(2).broadcast_to([P, chunks, P]),
                                  ALU.is_equal)
                dve.wait_ge(diff_ready, 2 * j + 2)
                dve.tensor_scalar(lo_hot[:, buf, 0:POOL_LO, :], lo_diff[:, buf, :, :], 0.0, None, ALU.is_equal)
                dve.tensor_scalar(hi_hot[:, buf, :, :], hi_diff[:, buf, :, :], 0.0, None,
                                  ALU.is_equal).then_inc(places_ready, 1)

            place_batch(0, 0, True)
            place_batch(1, 1, True)
            with dve.Fori(1, STEPS // 2) as m:
                for buf in range(2):
                    place_batch(2 * m + buf, buf, False)

            dve.wait_ge(deg_counted, STEPS)
            d, root, t1 = deg[:, 0, :], deg[:, 1, :], deg[:, 2, :]
            dve.tensor_scalar(d, ps[:, DEG_BANK, 0:TILES], 1.0, None, ALU.add).then_inc(deg_ready, 1)
            dve.wait_ge(sqrt_done, 1)
            link(dve.reciprocal(root, root))
            link(dve.tensor_tensor(t1, root, root, ALU.mult))
            link(dve.tensor_tensor(t1, t1, d, ALU.mult))
            link(dve.tensor_scalar(t1, t1, -0.5, 1.5, ALU.mult, ALU.add))
            dve.tensor_tensor(dinv[:, :], root, t1, ALU.mult).then_inc(dinv_ready, 1)

            dve.wait_ge(base_spread, 1)
            dve.wait_ge(w_copied, W_STEPS)
            link(dve.tensor_copy(group_base, ps[:, 4, 0:GROUPS]))
            link(dve.tensor_copy(group_int, group_base))
            link(dve.tensor_scalar(group_tile[:, :], group_int[0:1, :], 7, None, ALU.arith_shift_right))
            link(dve.tensor_scalar(group_int, group_int, P - 1, None, ALU.bitwise_and))
            link(dve.tensor_copy(group_place, group_int))
            link(dve.tensor_scalar(mask[:, 0, :], group_place, own_place[:, 0:1], None, ALU.is_le))
            dve.tensor_scalar(mask[:, 1, :], group_place, own_place[:, 0:1], None, ALU.is_gt).then_inc(groups_ready, 1)
            dve.wait_ge(groups_ready, 1)

            used = dst_f[:, 0:CHUNKS]

            def gap_to(firsts, n):
                return dve.tensor_tensor(order_gap.rearrange("p (g c) -> p g c", g=n), used.rearrange("p (g c) -> p g c", g=n),
                                         firsts.unsqueeze(2).broadcast_to([P, n, CHUNKS // n]), ALU.subtract)

            link(gap_to(group_base, GROUPS))
            link(dve.tensor_reduce(broken[:, 0:1], order_gap, AX.X, ALU.max))
            link(dve.tensor_reduce(broken[:, 1:2], order_gap, AX.X, ALU.min))
            link(gap_to(step_first[:, :], STEPS))
            link(dve.tensor_reduce(broken[:, 2:3], order_gap, AX.X, ALU.min))
            link(dve.tensor_tensor(broken[:, 3:4], broken[:, 1:2], broken[:, 2:3], ALU.min))
            link(dve.tensor_scalar(broken[:, 3:4], broken[:, 3:4], 0.0, None, ALU.is_lt))
            link(dve.tensor_scalar(broken[:, 0:1], broken[:, 0:1], float(P - 1), None, ALU.is_gt))
            dve.tensor_tensor(broken[:, 0:1], broken[:, 0:1], broken[:, 3:4], ALU.add).then_inc(order_checked, 1)
            dve.wait_ge(order_summed, 1)
            dve.tensor_copy(unordered[:, :], ps[0:1, ORDER_BANK, 0:1]).then_inc(path_known, 1)

            def stage_quad(quad, r):
                cols = bass.ds(CPQ * quad, CPQ)
                dve.tensor_copy(idx_stage[:, r * CPQ:(r + 1) * CPQ], src_idx[:, cols]).then_inc(idx_staged, 1)
                dve.tensor_tensor(onehot[:, r, :, :], place_iota[:, :].unsqueeze(1).broadcast_to([P, CPQ, P]),
                                  lo_f[:, cols].unsqueeze(2).broadcast_to([P, CPQ, P]), ALU.is_equal).then_inc(hot_ready, 1)

            def finish_quad(layer, i, r):
                dve.wait_ge(summed, layer * STEPS * QUADS + QUADS * i + (r + 1))
                if not is_static(i, STEPS - 1):
                    stage_quad(QUADS * i + (QUADS + r), r)
                elif layer < LAYERS - 1:
                    stage_quad(r, r)
                if r % GPS == GPS - 1:
                    add_group(layer, i, r * GPS // QUADS)

            def add_group(layer, i, bank):
                g = GPS * i + bank
                if not (layer == 0 and is_static(g, 0)):
                    dve.wait_ge(added, 2 * g + 2 * layer * GROUPS)
                t = dve.value_load(group_tile[0:1, bass.ds(g, 1)], min_val=0, max_val=TILES - 1)
                for part in range(2):
                    rows = tile_of(t + part)
                    dve.scalar_tensor_tensor(out=rows, in0=ps[:, bank, :], scalar=mask[:, part, bass.ds(g, 1)],
                                             in1=rows, op0=ALU.mult, op1=ALU.add).then_inc(added, 1)

            def bias_rows(layer, t):
                if layer == 0:
                    dve.wait_ge(tile_multiplied, t + 1)
                if not (layer == 0 and is_static(t, 0)):
                    dve.wait_ge(y_ready, layer * TILES + t)
                dve.scalar_tensor_tensor(out=h_sb[:, :], in0=ps[:, PRODUCT_BANK, :] if layer == 0 else tile_of(t),
                                         scalar=dinv[:, bass.ds(t, 1)], in1=bias[:, layer, :],
                                         op0=ALU.mult, op1=ALU.add).then_inc(h_ready, 1)

            def norm_rows(t):
                row = h_sb[:, :]
                done = LN_STEPS * t
                if not is_static(t, 0):
                    dve.wait_ge(o_ready, t)
                dve.wait_ge(x_loaded, 16 * t + 16)
                dve.scalar_tensor_tensor(out=row, in0=tile_of(t), scalar=dinv[:, bass.ds(t, 1)], in1=x_sb,
                                         op0=ALU.mult, op1=ALU.add).then_inc(ln_step, 1)
                dve.wait_ge(ln_step, done + 1)
                dve.tensor_tensor(row, row, bias[:, LAYERS - 1, :], ALU.add).then_inc(ln_step, 1)
                dve.wait_ge(ln_step, done + 2)
                dve.bn_stats(ln[:, 0:6], row).then_inc(ln_step, 1)
                stats_done = dve.to_reg(done + 3)
                dve.wait_ge(w_loaded, 16 * 6)
                dve.wait_ge(ln_step, stats_done)
                dve.bn_aggr(ln[:, 6:8], ln[:, 0:6]).then_inc(ln_step, 1)
                dve.wait_ge(ln_step, done + 4)
                dve.tensor_scalar(ln[:, 8:9], ln[:, 7:8], EPS, None, ALU.add).then_inc(ln_step, 1)
                dve.wait_ge(std_ready, t + 1)
                dve.reciprocal(ln[:, 10:11], ln[:, 9:10]).then_inc(ln_step, 1)
                dve.wait_ge(ln_step, done + 6)
                if not is_static(t, 0):
                    dve.wait_ge(o_stored, 16 * t)
                dve.tensor_scalar(row_sb[:, :], row, ln[:, 6:7], ln[:, 10:11], ALU.subtract, ALU.mult).then_inc(o_ready, 1)

            def rows(layer, t):
                if layer < LAYERS - 1:
                    bias_rows(layer, t)
                else:
                    norm_rows(t)

            def tiles_ready(layer):
                if layer == 0:
                    dve.wait_ge(y0_scaled, TILES)
                else:
                    dve.wait_ge(y_ready, TILES * layer)

            def step(layer, i, t):
                finish_quad(layer, i, 0)
                finish_quad(layer, i, 1)
                finish_quad(layer, i, 2)
                if t is not None:
                    rows(layer, t)
                finish_quad(layer, i, 3)

            def tail(layer, t):
                if is_static(t, STEPS - LAG):
                    dve.wait_ge(added, fast_done(layer, STEPS))
                rows(layer, t)

            def stage_any(i):
                dve.tensor_copy(idx_stage[:, :], src_idx[:, bass.ds(CPS * i, CPS)]).then_inc(any_staged, 1)

            def add_any(layer, i, t):
                n = TILES * i + t
                before = layer * STEPS * TILES
                dve.tensor_scalar(dst_off, dst_keep[:, bass.ds(CPS * i, CPS)], tile_first[:, bass.ds(t, 1)], None,
                                  ALU.subtract).then_inc(any_off, 1)
                dve.wait_ge(any_off, n + (before + 1))
                dve.tensor_tensor(onehot[:, :, :, :].rearrange("p q c n -> p (q c) n"),
                                  place_iota[:, :].unsqueeze(1).broadcast_to([P, CPS, P]),
                                  dst_off.unsqueeze(2).broadcast_to([P, CPS, P]), ALU.is_equal).then_inc(any_hot, 1)
                dve.wait_ge(any_summed, n + (before + 1))
                dve.wait_ge(any_added, n + (before + 1))
                dve.tensor_tensor(tile_of(t), tile_of(t), ps[:, 0, :], ALU.add).then_inc(any_added, 1)

            with order_holds(dve):
                for r in range(QUADS):
                    stage_quad(r, r)
                for layer in range(LAYERS):
                    tiles_ready(layer)
                    run_layer(dve, lambda i, t: step(layer, i, t), lambda t: tail(layer, t))
            with dve.Else():
                dve.tensor_copy(dst_keep, used).then_inc(any_added, 1)
                dve.wait_ge(any_added, 1)
                for layer in range(LAYERS):
                    tiles_ready(layer)
                    with dve.Fori(0, STEPS) as i:
                        stage_any(i)
                        with dve.Fori(0, TILES) as t:
                            add_any(layer, i, t)
                    dve.wait_ge(any_added, any_done(layer))
                    run_tiles(dve, lambda t: rows(layer, t))


_INS = ["x", "src", "dst", "L0_gnn_W1", "L0_gnn_b1", "L0_gnn_W2", "L0_gnn_b2", "L0_gnn_W3", "L0_gnn_b3"]


def kernel(**inputs):
    import concourse.bacc as bacc
    import numpy as np
    from concourse.bass_utils import run_bass_kernel_spmd

    nc = bacc.Bacc("TRN2", target_bir_lowering=False, num_devices=1)
    arrays, aps = {}, []
    for name in _INS:
        a = np.ascontiguousarray(inputs[name])
        arrays[f"in_{name}_dram"] = a
        aps.append(nc.dram_tensor(f"in_{name}_dram", a.shape, mybir.dt.from_np(a.dtype), kind="ExternalInput").ap())
    out = nc.dram_tensor("out_0_dram", inputs["x"].shape, F32, kind="ExternalOutput").ap()
    gcn_three_layers_resnorm(nc, *aps, out)
    result = run_bass_kernel_spmd(nc, [arrays], core_ids=[0])
    return result.results[0]["out_0_dram"]
```

```python
from contextlib import ExitStack

import concourse.bass as bass
from concourse import mybir

F32 = mybir.dt.float32
I32 = mybir.dt.int32
BF16 = mybir.dt.bfloat16
ALU = mybir.AluOpType
ACT = mybir.ActivationFunctionType
AX = mybir.AxisListType

P = 128
EPS = 1e-5
LAYERS = 3
CPQ = 4
QUADS = 4
CPS = CPQ * QUADS
GPS = 2
SPARE = 8 * P
LOW = 16
COUNTS = 8


def gcn_three_layers_resnorm(nc, x, src, dst, W1, b1, W2, b2, W3, b3, out):
    N, D = x.shape
    E = src.shape[0]
    FB = D // P
    TILES = -(-N // P)
    LAST = N - (TILES - 1) * P
    STEPS = -(-E // (P * CPS))
    GROUPS = STEPS * GPS
    CHUNKS = STEPS * CPS
    ROW_BLOCKS = -(-CHUNKS // P)
    COLS = ROW_BLOCKS * P
    FULL_ROWS = E // P
    FULL_BLOCKS = FULL_ROWS // P
    TAIL_ROWS = FULL_ROWS - FULL_BLOCKS * P
    TAIL_EDGES = E - FULL_ROWS * P
    X_BATCH = 4
    X_BATCHES = (TILES - 1) // X_BATCH
    LN_STEPS = 6
    W_STEPS = 4 * FB + 4
    CPG = CPS // GPS
    GPB = GROUPS // COUNTS
    CPB = GPB * CPG
    MIDS = 2 * P // LOW
    PADS = CHUNKS - -(-E // P)

    def lag_of(i):
        return 1 - (SPARE * N + i * P * (E - CPS * N)) // -(E * P)

    LAGS = sorted({lag_of(i) for i in range(STEPS)})
    PARTS = [(lag, min(i for i in range(STEPS) if lag_of(i) == lag),
              1 + max(i for i in range(STEPS) if lag_of(i) == lag)) for lag in LAGS]
    LOOP_TILES = STEPS - LAGS[-1]
    CONSTS = 7 + len(PARTS)
    assert LAGS == list(range(LAGS[0], LAGS[-1] + 1)) and [lag_of(i) for i in range(STEPS)] == sorted(map(lag_of, range(STEPS)))
    assert all(b - a > 2 for lag, a, b in PARTS) and PARTS[0][2] > LAGS[0] + 1 and LOOP_TILES == TILES - 2
    assert D == 512 and STEPS % 2 == 0 and LAST < P and TAIL_EDGES and PADS <= CPQ - 3
    assert (TILES - 1) % X_BATCH == 0 and FULL_BLOCKS + 1 == ROW_BLOCKS
    assert GROUPS % COUNTS == 0 and COUNTS % 2 == 0 and GPB * MIDS <= 256

    y_dram = [nc.dram_tensor(f"y{l}_dram", [N, D], F32, kind="Internal").ap() for l in range(LAYERS)]

    with ExitStack() as ctx:
        def sb(name, shape, dt):
            return ctx.enter_context(nc.sbuf_tensor(name, shape, dt))

        def sem(name):
            return ctx.enter_context(nc.semaphore(name))

        acc = sb("acc", [P, (TILES + 1) * D], F32)
        ring = sb("ring", [P, CPS, D], F32)
        onehot = sb("onehot", [P, QUADS, CPQ, P], F32)
        src_idx = sb("src_idx", [P, COLS], I32)
        lo_f = sb("lo_f", [P, COLS], F32)
        idx_stage = sb("idx_stage", [P, CPS], I32)
        mask = sb("mask", [P, 2, GROUPS], F32)
        group_tile = sb("group_tile", [1, GROUPS], I32)
        w123 = sb("w123", [P, FB, D], F32)
        w1_sb = sb("w1_sb", [P, FB, D], F32)
        w2_sb = sb("w2_sb", [P, FB, D], F32)
        w23 = sb("w23", [P, FB, D], F32)
        wT = sb("wT", [P, FB, D], F32)
        bias = sb("bias", [P, LAYERS, D], F32)
        row_sb = sb("row_sb", [P, D], F32)
        h_sb = sb("h_sb", [P, D], F32)
        ident = sb("ident", [P, P], F32)
        ones = sb("ones", [P, P], F32)
        place_iota = sb("place_iota", [P, P], F32)
        tile_iota = sb("tile_iota", [P, TILES], F32)
        own_place = sb("own_place", [P, 1], F32)
        step_first = sb("step_first", [P, STEPS], F32)
        tile_first = sb("tile_first", [P, TILES], F32)
        broken = sb("broken", [P, 4], F32)
        unordered = sb("unordered", [1, 1], I32)
        dinv = sb("dinv", [P, TILES], F32)
        deg = sb("deg", [P, 3, TILES], F32)
        ln = sb("ln", [P, 12], F32)

        w3_sb = w123
        x_sb = w1_sb[:, 0, :]
        turned_sb = w2_sb[:, 0, :]
        last_x = [w1_sb[:, 1 + k, :] for k in range(2)]
        last_turned = [w2_sb[:, 1 + k, :] for k in range(2)]
        last_h = [h_sb, row_sb]
        SPLIT = (0, 1, 1, 2)
        SPLIT_QUADS = sum(n > 0 for n in SPLIT)
        homes = [w[:, :, :].rearrange("p k n -> p (k n)") for w in (wT, w23, w1_sb)]
        home_cut = [0, 0, 0]

        def home(k, words):
            home_cut[k] += words
            return homes[k][:, home_cut[k] - words:home_cut[k]]

        def rows_home(k, n):
            return home(k, n * D).rearrange("p (c d) -> p c d", c=n)

        def part_home(k, n):
            return home(k, n * D // 2).bitcast(BF16).rearrange("p (c d) -> p c d", c=n)

        split_rest, split_parts = [None], [None]
        for kept_in in ((0, 0, 0, 0), (1, 1, 1, 1), (2, 2, 2, 0)):
            n = SPLIT[len(split_rest)]
            split_rest.append(rows_home(kept_in[0], n))
            split_parts.append([part_home(k, n) for k in kept_in[1:]])
        assert max(home_cut) <= FB * D
        split_hot = w2_sb[:, 3, 0:sum(SPLIT) * P // 2].bitcast(BF16).rearrange("p (s n) -> p s n", s=sum(SPLIT))
        hot_at = [sum(SPLIT[:r]) for r in range(QUADS)]
        last_row = [row_sb, w2_sb[:, 3, :]]

        tmp = ring[:, :, :].rearrange("p c d -> p (c d)")
        cut = [0]

        def carve(words):
            cut[0] += words
            return tmp[:, cut[0] - words:cut[0]]

        def places(chunks, width):
            return carve(2 * chunks * width // 2).bitcast(BF16).rearrange("p (b c n) -> p b c n", b=2, c=chunks)

        src_rows = carve(COLS)
        dst_f = carve(COLS)
        dst_rows = carve(COLS)
        dst_rel = carve(COLS).bitcast(I32)
        part_i = dst_rows.bitcast(I32)
        lists = carve(CHUNKS)
        low_list, mid_list = (lists[:, l * CHUNKS // 2:(l + 1) * CHUNKS // 2].bitcast(BF16) for l in range(2))
        order_gap = lists
        place_i = lists.bitcast(I32)
        group_base = carve(GROUPS)
        group_int = carve(GROUPS).bitcast(I32)
        group_place = carve(GROUPS)
        group_first = carve(GROUPS)

        def hots(rows):
            return carve(2 * rows * CPB // 2).bitcast(BF16).rearrange("p (b n c) -> p b n c", b=2, n=rows)

        low_hot = hots(LOW)
        mid_hot = hots(MIDS)
        assert cut[0] <= CPS * D
        counts = tmp[0:LOW, 2 * COLS:2 * COLS + GROUPS * MIDS]
        assert GROUPS * MIDS <= 2 * COLS
        counts_turned = h_sb[0:GROUPS, 0:2 * P]
        tile_hot = h_sb[0:GROUPS, 2 * P:2 * P + 2 * TILES].rearrange("g (k t) -> g k t", k=2)
        tile_col = h_sb[0:GROUPS, 2 * P + 2 * TILES:2 * P + 2 * TILES + 3]
        assert 2 * P + 2 * TILES + 3 <= D and GROUPS <= P
        cut[0] = 0
        any_int = carve(CHUNKS).bitcast(I32)
        any_tile = carve(CHUNKS)
        any_lo_hot = places(CPS, P)
        any_hi_hot = places(CPS, TILES)
        assert cut[0] <= CPS * D
        small = onehot[:, :, :, :].rearrange("p q c n -> p (q c n)")
        b_row = small[:, 0:2 * D].rearrange("p (l d) -> p l d", l=2)
        b_cols = small[:, 2 * D:4 * D].rearrange("p (l d) -> p l d", l=2)

        dst_keep = wT[:, 2:4, :].rearrange("p k n -> p (k n)")[:, 0:CHUNKS]
        dst_off = w23[:, 3, 0:CPS]

        ps = ctx.enter_context(nc.psum_tensor("ps", [P, 8, 512], F32))
        ORDER_BANK, TURN_BANK, PRODUCT_BANK, DEG_BANK = 4, 4, 5, 7
        LAST_TURN_BANK, LAST_PRODUCT_BANK = 6, 2
        GROUP_BANK = 4
        turned = ps[:, :, :].rearrange("p b n -> p (b n)")

        consts_ready = sem("consts_ready")
        pads_ready = sem("pads_ready")
        tail_zeroed = sem("tail_zeroed")
        dst_loaded = sem("dst_loaded")
        src_loaded = sem("src_loaded")
        w_loaded = sem("w_loaded")
        x_all_loaded = sem("x_all_loaded")
        dve_done = sem("dve_done")
        rows_float = sem("rows_float")
        edges_turned = sem("edges_turned")
        dst_ready = sem("dst_ready")
        base_spread = sem("base_spread")
        places_ready = sem("places_ready")
        deg_counted = sem("deg_counted")
        counts_copied = sem("counts_copied")
        counts_back = sem("counts_back")
        counts_ready = sem("counts_ready")
        tile_hot_ready = sem("tile_hot_ready")
        deg_merged = sem("deg_merged")
        deg_ready = sem("deg_ready")
        sqrt_done = sem("sqrt_done")
        dinv_ready = sem("dinv_ready")
        w_step = sem("w_step")
        w_copied = sem("w_copied")
        y0_scaled = sem("y0_scaled")
        y0_stored = sem("y0_stored")
        groups_ready = sem("groups_ready")
        order_checked = sem("order_checked")
        order_summed = sem("order_summed")
        path_known = sem("path_known")
        idx_staged = sem("idx_staged")
        hot_ready = sem("hot_ready")
        gathered = [sem(f"gathered{r}") for r in range(QUADS)]
        last_gathered = [sem(f"last_gathered{k}") for k in range(CPQ)]
        split_high = sem("split_high")
        split_less = sem("split_less")
        split_mid = sem("split_mid")
        split_ready = sem("split_ready")
        summed = sem("summed")
        added = sem("added")
        tile_staged = sem("tile_staged")
        tile_turned = sem("tile_turned")
        turn_copied = sem("turn_copied")
        tile_multiplied = sem("tile_multiplied")
        h_ready = sem("h_ready")
        y_ready = sem("y_ready")
        y_stored = sem("y_stored")
        x_loaded = sem("x_loaded")
        last_x_loaded = sem("last_x_loaded")
        ln_step = sem("ln_step")
        std_ready = sem("std_ready")
        o_ready = sem("o_ready")
        o_stored = sem("o_stored")

        any_places = sem("any_places")
        any_counted = sem("any_counted")
        any_staged = sem("any_staged")
        any_gathered = sem("any_gathered")
        any_off = sem("any_off")
        any_hot = sem("any_hot")
        any_summed = sem("any_summed")
        any_added = sem("any_added")

        block = ctx.enter_context(nc.Block())

        def run_layer(eng, step, tail):
            for lag, first, end in PARTS:
                if first == 0:
                    for i in range(lag):
                        step(i, None)
                    step(lag, 0)
                    start = lag + 1
                else:
                    step(first, None)
                    start = first + 1
                with eng.Fori(start, min(end, STEPS - 1)) as i:
                    step(i, i - lag)
            step(STEPS - 1, LOOP_TILES - 1)
            tail()

        def run_tiles(eng, work):
            work(0)
            with eng.Fori(1, TILES - 1) as t:
                work(t)
            work(TILES - 1)

        def order_holds(eng):
            eng.wait_ge(path_known, 1)
            return eng.If_eq(eng.to_reg(eng.value_load(unordered[0:1, 0:1])), 0)

        def fast_done(layer, i):
            return 2 * GPS * i + 2 * layer * GROUPS

        def any_done(layer):
            return (layer + 1) * STEPS * TILES + 1

        def split_rows(r):
            return ring[:, r * CPQ:r * CPQ + SPLIT[r], :]

        def wait_gathered(eng, layer, i, r):
            if is_static(i, STEPS - 1) and r == QUADS - 1:
                for k in range(max(SPLIT[r], 1)):
                    eng.wait_ge(last_gathered[k], 16 * (layer + 1))
            else:
                eng.wait_ge(gathered[r], 16 * CPQ * i + 16 * CPQ * (layer * (STEPS - (r == QUADS - 1)) + 1))

        def is_static(v, value):
            return isinstance(v, int) and v == value

        def rows_of(t):
            return LAST if is_static(t, TILES - 1) else P

        def node_rows(dram, t):
            return dram[bass.ds(P * t, rows_of(t)), :]

        def tile_of(t):
            return acc[:, bass.ds(D * t, D)]

        @block.sync
        def _(sp):
            tail_at = FULL_BLOCKS * P * P
            lists = ((dst_rows.bitcast(I32).rearrange("c (b p) -> c b p", p=P), dst, dst_loaded),
                     (src_rows.bitcast(I32).rearrange("c (b p) -> c b p", p=P), src, src_loaded))
            sp.wait_ge(pads_ready, 2)
            for r3, edges, loaded in lists:
                sp.dma_start(r3[:, 0:FULL_BLOCKS, :],
                             edges[0:tail_at].rearrange("(b c p) -> c b p", c=P, p=P)).then_inc(loaded, 16)
                sp.dma_start(r3[0:TAIL_ROWS, FULL_BLOCKS, :],
                             edges[tail_at:tail_at + TAIL_ROWS * P].rearrange("(c p) -> c p", p=P)).then_inc(loaded, 16)
                sp.dma_start(r3[TAIL_ROWS:TAIL_ROWS + 1, FULL_BLOCKS, 0:TAIL_EDGES],
                             edges[tail_at + TAIL_ROWS * P:E].rearrange("(c p) -> c p", c=1)).then_inc(loaded, 16)
            for t, w in ((w2_sb, W2), (w3_sb, W3), (w1_sb, W1)):
                sp.dma_start(t[:, :, :], w.rearrange("(k p) n -> p k n", p=P)).then_inc(w_loaded, 16)
            for l, b in enumerate((b1, b2)):
                sp.dma_start(b_row[0:1, l, :], b.rearrange("(a d) -> a d", a=1)).then_inc(w_loaded, 16)
            sp.dma_start(bias[:, 2, :], b3.rearrange("(a d) -> a d", a=1).broadcast_to([P, D])).then_inc(w_loaded, 16)

            whole = (TILES - 1) * P
            sp.dma_start(acc[:, 0:(TILES - 1) * D].rearrange("p (t d) -> p t d", d=D),
                         x[0:whole, :].rearrange("(t p) d -> p t d", p=P)).then_inc(x_all_loaded, 16)
            sp.wait_ge(tail_zeroed, 1)
            sp.dma_start(acc[0:LAST, (TILES - 1) * D:TILES * D], x[whole:N, :]).then_inc(x_all_loaded, 16)

            with sp.Fori(0, X_BATCHES) as k:
                sp.wait_ge(y0_scaled, X_BATCH * k + X_BATCH)
                sp.dma_start(y_dram[0][bass.ds(X_BATCH * P * k, X_BATCH * P), :].rearrange("(t p) d -> p t d", p=P),
                             acc[:, bass.ds(X_BATCH * D * k, X_BATCH * D)].rearrange("p (t d) -> p t d", d=D)
                             ).then_inc(y0_stored, 16)
            sp.wait_ge(y0_scaled, TILES)
            sp.dma_start(node_rows(y_dram[0], TILES - 1), acc[0:LAST, (TILES - 1) * D:TILES * D]).then_inc(y0_stored, 16)

            def store(layer, t):
                sp.wait_ge(y_ready, layer * TILES + t + 1)
                sp.dma_start(node_rows(y_dram[layer + 1], t), acc[0:rows_of(t), bass.ds(D * t, D)]).then_inc(y_stored, 16)

            def load_and_finish(t):
                if not is_static(t, 0):
                    sp.wait_ge(ln_step, LN_STEPS * t + (1 - LN_STEPS))
                sp.dma_start(x_sb[0:rows_of(t), :], node_rows(x, t)).then_inc(x_loaded, 16)
                sp.wait_ge(o_ready, t + 1)
                sp.dma_start(node_rows(out, t), row_sb[0:rows_of(t), :]).then_inc(o_stored, 16)

            def tile_work(layer, t):
                if t is not None:
                    if layer < LAYERS - 1:
                        store(layer, t)
                    else:
                        load_and_finish(t)

            def last_tiles(layer):
                for k in range(2):
                    t = LOOP_TILES + k
                    if layer < LAYERS - 1:
                        store(layer, t)
                    else:
                        sp.wait_ge(o_ready, t + 1)
                        sp.dma_start(node_rows(out, t), last_row[k][0:rows_of(t), :]).then_inc(o_stored, 16)

            with order_holds(sp):
                for layer in range(LAYERS):
                    if layer == LAYERS - 1:
                        for k in range(2):
                            t = LOOP_TILES + k
                            sp.dma_start(last_x[k][0:rows_of(t), :], node_rows(x, t)).then_inc(last_x_loaded, 16)
                    run_layer(sp, lambda i, t: tile_work(layer, t), lambda: last_tiles(layer))
            with sp.Else():
                for layer in range(LAYERS):
                    run_tiles(sp, lambda t: tile_work(layer, t))
            sp.wait_ge(o_stored, 16 * TILES)

        @block.gpsimd
        def _(pool):
            pads = slice(FULL_BLOCKS * P, COLS)
            pool.memset(dst_rows[:, pads].bitcast(I32), N).then_inc(pads_ready, 1)
            pool.memset(src_rows[:, pads].bitcast(I32), 0).then_inc(pads_ready, 1)
            pool.memset(ident[:, :], 0.0).then_inc(consts_ready, 1)
            pool.memset(ones[:, :], 1.0).then_inc(consts_ready, 1)
            pool.wait_ge(consts_ready, 2)
            pool.affine_select(out=ident[:, :], in_=ident[:, :], compare_op=ALU.not_equal, fill=1.0, base=0,
                               pattern=[[-1, P]], channel_multiplier=1).then_inc(consts_ready, 1)
            rows = [(place_iota[:, :], 1, P, 0, 0), (tile_iota[:, :], 1, TILES, 0, 0), (own_place[:, :], 1, 1, 0, 1),
                    (tile_first[:, :], P, TILES, 0, 0)]
            rows += [(step_first[:, a:b], P, b - a, P * (a - lag + 1), 0) for lag, a, b in PARTS]
            for row, by, width, base, down in rows:
                pool.iota(row, [[by, width]], base=base, channel_multiplier=down,
                          allow_small_or_imprecise_dtypes=True).then_inc(consts_ready, 1)
            pool.memset(acc[:, (TILES - 1) * D:], 0.0).then_inc(tail_zeroed, 1)

            def rows_stored(layer):
                if layer == 0:
                    pool.wait_ge(y0_stored, 16 * (X_BATCHES + 1))
                else:
                    pool.wait_ge(y_stored, 16 * TILES * layer)

            def gather(layer, s, landed):
                pool.indirect_dma_start(ring[:, s, :], None, y_dram[layer],
                                        bass.IndirectOffsetOnAxis(ap=idx_stage[:, s:s + 1], axis=0),
                                        bounds_check=N - 1, oob_is_err=False).then_inc(landed, 16)

            def gather_step(layer, i):
                for r in range(QUADS):
                    quad = pool.to_reg(layer * STEPS * QUADS + QUADS * i + (r + 1))
                    rows_stored(layer)
                    pool.wait_ge(idx_staged, quad)
                    if is_static(i, STEPS - 1) and r == QUADS - 1:
                        for k in range(CPQ - PADS):
                            gather(layer, r * CPQ + k, last_gathered[k])
                    else:
                        for k in range(CPQ):
                            gather(layer, r * CPQ + k, gathered[r])

            def gather_any(layer, i):
                turn = pool.to_reg(layer * STEPS + 1 + i)
                rows_stored(layer)
                pool.wait_ge(any_staged, turn)
                for s in range(CPS):
                    gather(layer, s, any_gathered)

            with order_holds(pool):
                for layer in range(LAYERS):
                    run_layer(pool, lambda i, t: gather_step(layer, i), lambda: None)
            with pool.Else():
                for layer in range(LAYERS):
                    with pool.Fori(0, STEPS) as i:
                        gather_any(layer, i)

        @block.tensor
        def _(pe):
            def turn_list(rows, at):
                for b in range(ROW_BLOCKS):
                    mm = pe.transpose(turned[:, at + b * P:at + (b + 1) * P], rows[:, b * P:(b + 1) * P], ident[:, :])
                mm.then_inc(edges_turned, 1)

            pe.wait_ge(consts_ready, CONSTS)
            pe.wait_ge(rows_float, 1)
            turn_list(dst_rows, 0)
            pe.wait_ge(dst_ready, 1)
            firsts = dst_f[0:1, 0:CHUNKS:CPG]
            pe.matmul(ps[:, GROUP_BANK, 0:GROUPS], ones[0:1, :], firsts, start=True, stop=True)
            pe.matmul(ps[0:GROUPS, GROUP_BANK, GROUPS:GROUPS + 1], firsts, ones[0:1, 0:1],
                      start=True, stop=True).then_inc(base_spread, 1)

            def count_batch(j, buf):
                pe.wait_ge(places_ready, j + 1)
                for g in range(GPB):
                    for k in range(CPG):
                        mm = pe.matmul(turned[0:LOW, bass.ds(256 * j + g * MIDS, MIDS)], low_hot[:, buf, :, g * CPG + k],
                                       mid_hot[:, buf, :, g * CPG + k], start=(k == 0), stop=(k == CPG - 1),
                                       skip_group_check=True)
                mm.then_inc(deg_counted, 1)

            def merge_counts():
                pe.wait_ge(counts_copied, 1)
                for m in range(MIDS):
                    mm = pe.transpose(ps[0:GROUPS, GROUP_BANK, 256 + m * LOW:256 + (m + 1) * LOW],
                                      counts[:, m:GROUPS * MIDS:MIDS], ident[0:LOW, 0:LOW])
                mm.then_inc(counts_back, 1)
                pe.wait_ge(tile_hot_ready, 1)
                pe.wait_ge(counts_ready, 1)
                for part in range(2):
                    mm = pe.matmul(ps[:, DEG_BANK, 0:TILES], counts_turned[:, part * P:(part + 1) * P], tile_hot[:, part, :],
                                   start=(part == 0), stop=(part == 1))
                mm.then_inc(deg_merged, 1)

            def count_any(j, buf, first, last):
                pe.wait_ge(any_places, j + 1)
                for k in range(CPS):
                    mm = pe.matmul(ps[:, DEG_BANK, 0:TILES], any_lo_hot[:, buf, k, :], any_hi_hot[:, buf, k, :],
                                   start=(first and k == 0), stop=(last and k == CPS - 1), skip_group_check=True)
                mm.then_inc(any_counted, 1)

            at = [0]

            def weight_bank(needs):
                k = at[0]
                at[0] += 1
                if max(needs, k - 1) > 0:
                    pe.wait_ge(w_copied, max(needs, k - 1))
                return ps[:, 5 + k % 2, :]

            def turn_weight(w, j):
                bank = weight_bank(0)
                for i in range(FB):
                    mm = pe.transpose(bank[:, i * P:(i + 1) * P], w[:, i, j * P:(j + 1) * P], ident[:, :])
                mm.then_inc(w_step, 1)

            def product(lhs, rhs, needs):
                bank = weight_bank(needs)
                for k in range(FB):
                    mm = pe.matmul(bank, lhs(k), rhs[:, k, :], start=(k == 0), stop=(k == FB - 1))
                mm.then_inc(w_step, 1)

            def spread_bias(l):
                bank = weight_bank(0)
                for k in range(FB):
                    mm = pe.matmul(bank[:, k * P:(k + 1) * P], b_row[0:1, l, k * P:(k + 1) * P], ones[0:1, :],
                                   start=True, stop=True)
                mm.then_inc(w_step, 1)

            def weight_step(k):
                if k < FB:
                    turn_weight(w2_sb, k)
                elif k < 2 * FB:
                    product(lambda j: wT[:, j, (k - FB) * P:(k - FB + 1) * P], w3_sb, FB)
                elif k < 2 * FB + 2:
                    spread_bias(k - 2 * FB)
                elif k < 2 * FB + 4:
                    l = k - 2 * FB - 2
                    product(lambda j: b_cols[:, l, j * P:(j + 1) * P], (w23, w3_sb)[l], 2 * FB + 2)
                elif k < 3 * FB + 4:
                    turn_weight(w1_sb, k - 2 * FB - 4)
                else:
                    i = k - 3 * FB - 4
                    product(lambda j: wT[:, j, i * P:(i + 1) * P], w23, 3 * FB + 4)

            pe.wait_ge(w_loaded, 16 * 6)
            for k in range(FB):
                weight_step(k)
            with pe.Fori(0, COUNTS // 2) as m:
                for buf in range(2):
                    count_batch(2 * m + buf, buf)
            merge_counts()

            pe.wait_ge(order_checked, 1)
            pe.matmul(ps[0:1, ORDER_BANK, 0:1], broken[:, 0:1], ones[:, 0:1], start=True, stop=True).then_inc(order_summed, 1)

            pe.wait_ge(rows_float, 2)
            turn_list(src_rows, 1024)

            for k in range(FB, W_STEPS):
                weight_step(k)

            def sum_quad(layer, i, r):
                bank = r * GPS // QUADS
                pe.wait_ge(hot_ready, layer * STEPS * QUADS + QUADS * i + (r + 1))
                last = is_static(i, STEPS - 1) and r == QUADS - 1
                wait_gathered(pe, layer, i, r)
                opens, closes = r % GPS == 0, r % GPS == GPS - 1
                if opens and not (layer == 0 and is_static(i, 0)):
                    pe.wait_ge(added, 2 * GPS * i + 2 * (layer * GROUPS + bank + 1 - GPS))
                chunks = CPQ - PADS if last else CPQ
                splits = SPLIT[r] if layer == 0 else 0
                for k in range(splits, chunks):
                    if last and k > 0:
                        pe.wait_ge(last_gathered[k], 16 * (layer + 1))
                    mm = pe.matmul(ps[:, bank, :], onehot[:, r, k, :], ring[:, r * CPQ + k, :],
                                   start=(opens and k == splits), stop=(closes and k == chunks - 1 and not splits),
                                   skip_group_check=True)
                if splits:
                    pe.wait_ge(split_ready, SPLIT_QUADS * i + r)
                    for k in range(splits):
                        for n, rows in enumerate(split_parts[r]):
                            mm = pe.matmul(ps[:, bank, :], split_hot[:, hot_at[r] + k, :], rows[:, k, :], start=False,
                                           stop=(closes and k == splits - 1 and n == 2), skip_group_check=True)
                mm.then_inc(summed, 1)

            def turn_tile(t):
                pe.wait_ge(tile_staged, t + 1)
                if not is_static(t, 0):
                    pe.wait_ge(turn_copied, t)
                for k in range(FB):
                    mm = pe.transpose(ps[:, TURN_BANK, k * P:(k + 1) * P], row_sb[:, k * P:(k + 1) * P], ident[:, :])
                mm.then_inc(tile_turned, 1)

            def multiply_tile(t):
                pe.wait_ge(turn_copied, t + 1)
                if not is_static(t, 0):
                    pe.wait_ge(h_ready, t)
                for k in range(FB):
                    mm = pe.matmul(ps[:, PRODUCT_BANK, :], turned_sb[:, k * P:(k + 1) * P], w123[:, k, :],
                                   start=(k == 0), stop=(k == FB - 1))
                mm.then_inc(tile_multiplied, 1)

            def step(layer, i, t):
                sum_quad(layer, i, 0)
                sum_quad(layer, i, 1)
                if layer == 0 and t is not None:
                    turn_tile(t)
                sum_quad(layer, i, 2)
                if layer == 0 and t is not None:
                    multiply_tile(t)
                sum_quad(layer, i, 3)

            def last_tiles(layer):
                if layer > 0:
                    return
                pe.wait_ge(added, fast_done(layer, STEPS))
                for j in range(2):
                    rows = tile_of(LOOP_TILES + j)
                    for k in range(FB):
                        mm = pe.transpose(ps[:, LAST_TURN_BANK + j, k * P:(k + 1) * P], rows[:, k * P:(k + 1) * P], ident[:, :])
                    mm.then_inc(tile_turned, 1)
                for j in range(2):
                    pe.wait_ge(turn_copied, LOOP_TILES + j + 1)
                    for k in range(FB):
                        mm = pe.matmul(ps[:, LAST_PRODUCT_BANK + j, :], last_turned[j][:, k * P:(k + 1) * P], w123[:, k, :],
                                       start=(k == 0), stop=(k == FB - 1))
                    mm.then_inc(tile_multiplied, 1)

            def any_tile_product(t):
                turn_tile(t)
                multiply_tile(t)

            def sum_any(layer, i, t):
                pe.wait_ge(any_gathered, 16 * CPS * i + 16 * CPS * (layer * STEPS + 1))
                pe.wait_ge(any_hot, TILES * i + t + (layer * STEPS * TILES + 1))
                for s in range(CPS):
                    mm = pe.matmul(ps[:, 0, :], onehot[:, s // CPQ, s % CPQ, :], ring[:, s, :],
                                   start=(s == 0), stop=(s == CPS - 1))
                mm.then_inc(any_summed, 1)

            with order_holds(pe):
                for layer in range(LAYERS):
                    run_layer(pe, lambda i, t: step(layer, i, t), lambda: last_tiles(layer))
            with pe.Else():
                count_any(0, 0, True, False)
                count_any(1, 1, False, False)
                with pe.Fori(1, STEPS // 2 - 1) as m:
                    for buf in range(2):
                        count_any(2 * m + buf, buf, False, False)
                count_any(STEPS - 2, 0, False, False)
                count_any(STEPS - 1, 1, False, True)
                for layer in range(LAYERS):
                    with pe.Fori(0, STEPS) as i:
                        with pe.Fori(0, TILES) as t:
                            sum_any(layer, i, t)
                    if layer == 0:
                        run_tiles(pe, any_tile_product)

        @block.scalar
        def _(act):
            act.wait_ge(edges_turned, 1)
            act.copy(dst_f, turned[:, 0:COLS]).then_inc(dst_ready, 1)

            dests = ([wT[:, k, :] for k in range(FB)] + [w23[:, k, :] for k in range(FB)]
                     + [b_cols[:, l, :] for l in range(2)] + [bias[:, l, :] for l in range(2)]
                     + [wT[:, k, :] for k in range(FB)] + [w123[:, k, :] for k in range(FB)])

            def copy_weights(a, b):
                for k in range(a, b):
                    act.wait_ge(w_step, k + 1)
                    act.copy(dests[k], ps[:, 5 + k % 2, :]).then_inc(w_copied, 1)

            copy_weights(0, FB)
            act.wait_ge(deg_counted, COUNTS)
            act.copy(counts.rearrange("p (b n) -> p b n", b=COUNTS),
                     turned[0:LOW, 0:256 * COUNTS].rearrange("p (b n) -> p b n", b=COUNTS)[:, :, 0:GPB * MIDS]
                     ).then_inc(counts_copied, 1)
            act.wait_ge(counts_back, 1)
            act.copy(counts_turned, ps[0:GROUPS, GROUP_BANK, 256:512]).then_inc(counts_ready, 1)

            def root():
                act.wait_ge(deg_ready, 1)
                act.activation(deg[:, 1, :], deg[:, 0, :], ACT.Sqrt).then_inc(sqrt_done, 1)

            def stage_rows(t):
                if not is_static(t, 0):
                    act.wait_ge(tile_turned, t)
                act.activation(row_sb[:, :], tile_of(t), ACT.Copy).then_inc(tile_staged, 1)

            def keep_turned(t):
                act.wait_ge(tile_turned, t + 1)
                if not is_static(t, 0):
                    act.wait_ge(tile_multiplied, t)
                act.activation(turned_sb, ps[:, TURN_BANK, :], ACT.Copy).then_inc(turn_copied, 1)

            def scale_rows(layer, t, h=h_sb):
                act.wait_ge(h_ready, layer * TILES + t + 1)
                act.activation(tile_of(t), h[:, :], ACT.Copy, scale=dinv[:, bass.ds(t, 1)]).then_inc(y_ready, 1)

            def std(t):
                act.wait_ge(ln_step, LN_STEPS * t + 5)
                act.activation(ln[:, 9:10], ln[:, 8:9], ACT.Sqrt).then_inc(std_ready, 1)

            def work(layer, t, sums, count):
                if t is None:
                    return
                if layer == 0:
                    act.wait_ge(sums, count)
                    stage_rows(t)
                    keep_turned(t)
                if layer < LAYERS - 1:
                    scale_rows(layer, t)
                else:
                    std(t)

            def split_quad(i, r):
                high, mid, low = split_parts[r]
                n = act.to_reg(SPLIT_QUADS * i + r)
                wait_gathered(act, 0, i, r)
                act.activation(high, split_rows(r), ACT.Copy).then_inc(split_high, 1)
                act.wait_ge(w_copied, W_STEPS)
                act.wait_ge(split_less, n)
                act.activation(mid, split_rest[r], ACT.Copy).then_inc(split_mid, 1)

            def first_layer_step(i, t):
                split_quad(i, 1)
                if t is not None:
                    act.wait_ge(added, fast_done(0, i))
                    stage_rows(t)
                split_quad(i, 2)
                if t is not None:
                    keep_turned(t)
                split_quad(i, 3)
                if t is not None:
                    scale_rows(0, t)

            def fast_step(layer, i, t):
                if layer == 0:
                    first_layer_step(i, t)
                else:
                    work(layer, t, added, fast_done(layer, i))

            def last_tiles(layer):
                if layer == 0:
                    for k in range(2):
                        act.wait_ge(tile_turned, LOOP_TILES + k + 1)
                        act.activation(last_turned[k], ps[:, LAST_TURN_BANK + k, :], ACT.Copy).then_inc(turn_copied, 1)
                for k in range(2):
                    if layer < LAYERS - 1:
                        scale_rows(layer, LOOP_TILES + k, last_h[k])
                    else:
                        std(LOOP_TILES + k)

            with order_holds(act):
                root()
                copy_weights(FB, W_STEPS)
                act.wait_ge(dinv_ready, 1)
                for layer in range(LAYERS):
                    run_layer(act, lambda i, t: fast_step(layer, i, t), lambda: last_tiles(layer))
            with act.Else():
                copy_weights(FB, W_STEPS)
                root()
                act.wait_ge(dinv_ready, 1)
                for layer in range(LAYERS):
                    run_tiles(act, lambda t: work(layer, t, any_added, any_done(layer)))

        @block.vector
        def _(dve):
            count = [0]

            def link(ins):
                count[0] += 1
                ins.then_inc(dve_done, 1)
                dve.wait_ge(dve_done, count[0])

            dve.wait_ge(dst_loaded, 16 * 3)
            dve.tensor_copy(dst_rows, dst_rows.bitcast(I32)).then_inc(rows_float, 1)

            used = dst_f[:, 0:CHUNKS]
            rel = dst_rel[:, 0:CHUNKS]
            part = part_i[:, 0:CHUNKS]
            dve.wait_ge(base_spread, 1)
            tile_int = tile_col[:, 0:1].bitcast(I32)
            dve.tensor_copy(tile_int, ps[0:GROUPS, GROUP_BANK, GROUPS:GROUPS + 1])
            link(dve.tensor_copy(group_base, ps[:, GROUP_BANK, 0:GROUPS]))
            link(dve.tensor_copy(group_int, group_base))
            link(dve.tensor_scalar(group_place.bitcast(I32), group_int, 7, None, ALU.arith_shift_right))
            link(dve.tensor_scalar(group_first, group_place.bitcast(I32), float(P), None, ALU.mult))
            link(dve.tensor_tensor(rel.rearrange("p (g c) -> p g c", c=CPG), used.rearrange("p (g c) -> p g c", c=CPG),
                                   group_first.unsqueeze(2).broadcast_to([P, GROUPS, CPG]), ALU.subtract))
            link(dve.tensor_scalar(part, rel, LOW - 1, None, ALU.bitwise_and))
            dve.tensor_copy(low_list, part)
            link(dve.tensor_scalar(rel, rel, LOW.bit_length() - 1, None, ALU.arith_shift_right))
            link(dve.tensor_copy(mid_list, rel))

            def place_batch(j, buf, first):
                if not first:
                    dve.wait_ge(deg_counted, j - 1)
                for hot, values, rows in ((low_hot, low_list, LOW), (mid_hot, mid_list, MIDS)):
                    for n in range(rows):
                        one = dve.tensor_scalar(hot[:, buf, n, :], values[:, bass.ds(CPB * j, CPB)], float(n), None, ALU.is_equal)
                one.then_inc(places_ready, 1)

            place_batch(0, 0, True)
            place_batch(1, 1, True)
            with dve.Fori(1, COUNTS // 2) as m:
                for buf in range(2):
                    place_batch(2 * m + buf, buf, False)

            dve.wait_ge(consts_ready, CONSTS)
            link(dve.tensor_scalar(tile_int, tile_int, 7, None, ALU.arith_shift_right))
            link(dve.tensor_copy(tile_col[:, 1:2], tile_int))
            link(dve.tensor_scalar(tile_col[:, 2:3], tile_col[:, 1:2], 1.0, None, ALU.add))
            dve.tensor_scalar(tile_hot[:, 0, :], tile_iota[0:GROUPS, :], tile_col[:, 1:2], None, ALU.is_equal)
            dve.tensor_scalar(tile_hot[:, 1, :], tile_iota[0:GROUPS, :], tile_col[:, 2:3], None,
                              ALU.is_equal).then_inc(tile_hot_ready, 1)

            def gap_to(firsts, n):
                return dve.tensor_tensor(order_gap.rearrange("p (g c) -> p g c", g=n), used.rearrange("p (g c) -> p g c", g=n),
                                         firsts.unsqueeze(2).broadcast_to([P, n, CHUNKS // n]), ALU.subtract)

            link(gap_to(group_base, GROUPS))
            link(dve.tensor_reduce(broken[:, 0:1], order_gap, AX.X, ALU.max))
            link(dve.tensor_reduce(broken[:, 1:2], order_gap, AX.X, ALU.min))
            link(gap_to(step_first[:, :], STEPS))
            link(dve.tensor_reduce(broken[:, 2:3], order_gap, AX.X, ALU.min))
            link(dve.tensor_tensor(broken[:, 3:4], broken[:, 1:2], broken[:, 2:3], ALU.min))
            link(dve.tensor_scalar(broken[:, 3:4], broken[:, 3:4], 0.0, None, ALU.is_lt))
            link(dve.tensor_scalar(broken[:, 0:1], broken[:, 0:1], float(P - 1), None, ALU.is_gt))
            dve.tensor_tensor(broken[:, 0:1], broken[:, 0:1], broken[:, 3:4], ALU.add).then_inc(order_checked, 1)
            dve.wait_ge(src_loaded, 16 * 3)
            dve.tensor_copy(src_rows, src_rows.bitcast(I32)).then_inc(rows_float, 1)
            dve.wait_ge(order_summed, 1)
            dve.tensor_copy(unordered[:, :], ps[0:1, ORDER_BANK, 0:1]).then_inc(path_known, 1)

            def keep_edges():
                link(dve.tensor_copy(place_i, used))
                link(dve.tensor_scalar(place_i, place_i, P - 1, None, ALU.bitwise_and))
                link(dve.tensor_copy(lo_f[:, 0:CHUNKS], place_i))
                dve.wait_ge(edges_turned, 2)
                link(dve.tensor_copy(src_idx[:, :], turned[:, 1024:1024 + COLS]))

            def keep_groups():
                link(dve.tensor_scalar(group_tile[:, :], group_int[0:1, :], 7, None, ALU.arith_shift_right))
                link(dve.tensor_scalar(group_int, group_int, P - 1, None, ALU.bitwise_and))
                link(dve.tensor_copy(group_place, group_int))
                link(dve.tensor_scalar(mask[:, 0, :], group_place, own_place[:, 0:1], None, ALU.is_le))
                dve.tensor_scalar(mask[:, 1, :], group_place, own_place[:, 0:1], None, ALU.is_gt).then_inc(groups_ready, 1)
                dve.wait_ge(groups_ready, 1)

            def invert_degrees():
                d, root, t1 = deg[:, 0, :], deg[:, 1, :], deg[:, 2, :]
                dve.tensor_scalar(d, ps[:, DEG_BANK, 0:TILES], 1.0, None, ALU.add).then_inc(deg_ready, 1)
                dve.wait_ge(sqrt_done, 1)
                link(dve.reciprocal(root, root))
                link(dve.tensor_tensor(t1, root, root, ALU.mult))
                link(dve.tensor_tensor(t1, t1, d, ALU.mult))
                link(dve.tensor_scalar(t1, t1, -0.5, 1.5, ALU.mult, ALU.add))
                dve.tensor_tensor(dinv[:, :], root, t1, ALU.mult).then_inc(dinv_ready, 1)

            def scale_x():
                dve.wait_ge(dinv_ready, 1)
                dve.wait_ge(x_all_loaded, 32)

                def scale(t):
                    dve.tensor_scalar(tile_of(t), tile_of(t), dinv[:, bass.ds(t, 1)], None, ALU.mult).then_inc(y0_scaled, 1)

                with dve.Fori(0, X_BATCHES) as k:
                    for r in range(X_BATCH):
                        scale(X_BATCH * k + r)
                scale(TILES - 1)

            def place_any(j, buf, first):
                if not first:
                    dve.wait_ge(any_counted, j - 1)
                for hot, iota, values, width in ((any_lo_hot, place_iota, lo_f, P), (any_hi_hot, tile_iota, any_tile, TILES)):
                    one = dve.tensor_tensor(hot[:, buf, :, :], iota[:, :].unsqueeze(1).broadcast_to([P, CPS, width]),
                                            values[:, bass.ds(CPS * j, CPS)].unsqueeze(2).broadcast_to([P, CPS, width]),
                                            ALU.is_equal)
                one.then_inc(any_places, 1)

            def stage_indices(quad, r):
                dve.tensor_copy(idx_stage[:, r * CPQ:(r + 1) * CPQ],
                                src_idx[:, bass.ds(CPQ * quad, CPQ)]).then_inc(idx_staged, 1)

            def stage_places(layer, quad, r):
                splits = SPLIT[r] if layer == 0 else 0
                for k in range(splits):
                    dve.tensor_scalar(split_hot[:, hot_at[r] + k, :], place_iota[:, :], lo_f[:, bass.ds(CPQ * quad + k, 1)],
                                      None, ALU.is_equal)
                chunks = CPQ - splits
                dve.tensor_tensor(onehot[:, r, splits:CPQ, :], place_iota[:, :].unsqueeze(1).broadcast_to([P, chunks, P]),
                                  lo_f[:, bass.ds(CPQ * quad + splits, chunks)].unsqueeze(2).broadcast_to([P, chunks, P]),
                                  ALU.is_equal).then_inc(hot_ready, 1)

            def stage_quad(layer, quad, r):
                stage_indices(quad, r)
                stage_places(layer, quad, r)

            def split_less_high(i, r):
                n = dve.to_reg(SPLIT_QUADS * i + r)
                dve.wait_ge(path_known, 1)
                dve.wait_ge(split_high, n)
                dve.tensor_tensor(split_rest[r], split_rows(r), split_parts[r][0], ALU.subtract).then_inc(split_less, 1)

            def split_less_mid(i, r):
                n = dve.to_reg(SPLIT_QUADS * i + r)
                dve.wait_ge(path_known, 1)
                dve.wait_ge(split_mid, n)
                dve.tensor_tensor(split_parts[r][2], split_rest[r], split_parts[r][1], ALU.subtract).then_inc(split_ready, 1)

            def finish_quad(layer, i, r):
                dve.wait_ge(summed, layer * STEPS * QUADS + QUADS * i + (r + 1))
                closes = r % (QUADS // GPS) == QUADS // GPS - 1
                if not is_static(i, STEPS - 1):
                    stage_quad(layer, QUADS * i + (QUADS + r), r)
                if closes:
                    add_group(layer, i, r * GPS // QUADS)
                if is_static(i, STEPS - 1) and layer < LAYERS - 1 and r < QUADS - 1:
                    stage_quad(layer + 1, r, r)

            def add_group(layer, i, bank):
                g = GPS * i + bank
                if not (layer == 0 and is_static(g, 0)):
                    dve.wait_ge(added, 2 * g + 2 * layer * GROUPS)
                t = dve.value_load(group_tile[0:1, bass.ds(g, 1)], min_val=0, max_val=TILES - 1)
                for part in range(2):
                    rows = tile_of(t + part)
                    dve.scalar_tensor_tensor(out=rows, in0=ps[:, bank, :], scalar=mask[:, part, bass.ds(g, 1)],
                                             in1=rows, op0=ALU.mult, op1=ALU.add).then_inc(added, 1)

            def bias_rows(layer, t, h=h_sb, bank=PRODUCT_BANK):
                if layer == 0:
                    dve.wait_ge(tile_multiplied, t + 1)
                if h is h_sb and not (layer == 0 and is_static(t, 0)):
                    dve.wait_ge(y_ready, layer * TILES + t)
                dve.scalar_tensor_tensor(out=h[:, :], in0=ps[:, bank, :] if layer == 0 else tile_of(t),
                                         scalar=dinv[:, bass.ds(t, 1)], in1=bias[:, layer, :],
                                         op0=ALU.mult, op1=ALU.add).then_inc(h_ready, 1)

            def norm_rows(t, last=None):
                row = h_sb[:, :]
                done = LN_STEPS * t
                if not is_static(t, 0):
                    dve.wait_ge(o_ready, t)
                if last is None:
                    dve.wait_ge(x_loaded, 16 * t + 16)
                elif last == 0:
                    dve.wait_ge(last_x_loaded, 32)
                dve.scalar_tensor_tensor(out=row, in0=tile_of(t), scalar=dinv[:, bass.ds(t, 1)],
                                         in1=x_sb if last is None else last_x[last],
                                         op0=ALU.mult, op1=ALU.add).then_inc(ln_step, 1)
                dve.wait_ge(ln_step, done + 1)
                dve.tensor_tensor(row, row, bias[:, LAYERS - 1, :], ALU.add).then_inc(ln_step, 1)
                dve.wait_ge(ln_step, done + 2)
                dve.bn_stats(ln[:, 0:6], row).then_inc(ln_step, 1)
                stats_done = dve.to_reg(done + 3)
                dve.wait_ge(w_loaded, 16 * 6)
                dve.wait_ge(ln_step, stats_done)
                dve.bn_aggr(ln[:, 6:8], ln[:, 0:6]).then_inc(ln_step, 1)
                dve.wait_ge(ln_step, done + 4)
                dve.tensor_scalar(ln[:, 8:9], ln[:, 7:8], EPS, None, ALU.add).then_inc(ln_step, 1)
                dve.wait_ge(std_ready, t + 1)
                dve.reciprocal(ln[:, 10:11], ln[:, 9:10]).then_inc(ln_step, 1)
                dve.wait_ge(ln_step, done + 6)
                if last != 1 and not is_static(t, 0):
                    dve.wait_ge(o_stored, 16 * t)
                dve.tensor_scalar(row_sb[:, :] if last is None else last_row[last][:, :], row, ln[:, 6:7], ln[:, 10:11], ALU.subtract, ALU.mult).then_inc(o_ready, 1)

            def rows(layer, t):
                if layer < LAYERS - 1:
                    bias_rows(layer, t)
                else:
                    norm_rows(t)

            def tiles_ready(layer):
                if layer == 0:
                    dve.wait_ge(y0_scaled, TILES)
                else:
                    dve.wait_ge(y_ready, TILES * layer)

            def step(layer, i, t):
                early = layer == LAYERS - 1 and is_static(i, STEPS - 1)
                if layer == 0:
                    for r in range(1, QUADS):
                        split_less_high(i, r)
                        split_less_mid(i, r)
                        finish_quad(layer, i, r - 1)
                else:
                    finish_quad(layer, i, 0)
                    if early:
                        rows(layer, t)
                    finish_quad(layer, i, 1)
                    finish_quad(layer, i, 2)
                if t is not None and not early:
                    rows(layer, t)
                finish_quad(layer, i, 3)

            def last_tiles(layer):
                dve.wait_ge(added, fast_done(layer, STEPS))
                for k in range(2):
                    t = LOOP_TILES + k
                    if layer < LAYERS - 1:
                        bias_rows(layer, t, last_h[k], LAST_PRODUCT_BANK + k)
                    else:
                        norm_rows(t, k)
                if layer < LAYERS - 1:
                    stage_quad(layer + 1, QUADS - 1, QUADS - 1)

            def stage_any(i):
                dve.tensor_copy(idx_stage[:, :], src_idx[:, bass.ds(CPS * i, CPS)]).then_inc(any_staged, 1)

            def add_any(layer, i, t):
                n = TILES * i + t
                before = layer * STEPS * TILES
                dve.tensor_scalar(dst_off, dst_keep[:, bass.ds(CPS * i, CPS)], tile_first[:, bass.ds(t, 1)], None,
                                  ALU.subtract).then_inc(any_off, 1)
                dve.wait_ge(any_off, n + (before + 1))
                dve.tensor_tensor(onehot[:, :, :, :].rearrange("p q c n -> p (q c) n"),
                                  place_iota[:, :].unsqueeze(1).broadcast_to([P, CPS, P]),
                                  dst_off.unsqueeze(2).broadcast_to([P, CPS, P]), ALU.is_equal).then_inc(any_hot, 1)
                dve.wait_ge(any_summed, n + (before + 1))
                dve.wait_ge(any_added, n + (before + 1))
                dve.tensor_tensor(tile_of(t), tile_of(t), ps[:, 0, :], ALU.add).then_inc(any_added, 1)

            linked = count[0]
            with order_holds(dve):
                dve.wait_ge(deg_merged, 1)
                invert_degrees()
                scale_x()
                keep_edges()
                keep_groups()
                for r in range(QUADS):
                    stage_indices(r, r)
                dve.wait_ge(w_copied, 2 * FB + 4)
                for r in range(QUADS):
                    stage_places(0, r, r)
                for layer in range(LAYERS):
                    tiles_ready(layer)
                    run_layer(dve, lambda i, t: step(layer, i, t), lambda: last_tiles(layer))
            with dve.Else():
                count[0] = linked
                dve.wait_ge(w_copied, W_STEPS)
                dve.tensor_copy(dst_keep, used).then_inc(any_added, 1)
                dve.wait_ge(any_added, 1)
                keep_edges()
                link(dve.tensor_copy(any_int, dst_keep))
                link(dve.tensor_scalar(any_int, any_int, 7, None, ALU.arith_shift_right))
                link(dve.tensor_copy(any_tile, any_int))
                place_any(0, 0, True)
                place_any(1, 1, True)
                with dve.Fori(1, STEPS // 2) as m:
                    for buf in range(2):
                        place_any(2 * m + buf, buf, False)
                dve.wait_ge(any_counted, STEPS)
                invert_degrees()
                scale_x()
                for layer in range(LAYERS):
                    tiles_ready(layer)
                    with dve.Fori(0, STEPS) as i:
                        stage_any(i)
                        with dve.Fori(0, TILES) as t:
                            add_any(layer, i, t)
                    dve.wait_ge(any_added, any_done(layer))
                    run_tiles(dve, lambda t: rows(layer, t))


_INS = ["x", "src", "dst", "L0_gnn_W1", "L0_gnn_b1", "L0_gnn_W2", "L0_gnn_b2", "L0_gnn_W3", "L0_gnn_b3"]


def kernel(**inputs):
    import concourse.bacc as bacc
    import numpy as np
    from concourse.bass_utils import run_bass_kernel_spmd

    nc = bacc.Bacc("TRN2", target_bir_lowering=False, num_devices=1)
    arrays, aps = {}, []
    for name in _INS:
        a = np.ascontiguousarray(inputs[name])
        arrays[f"in_{name}_dram"] = a
        aps.append(nc.dram_tensor(f"in_{name}_dram", a.shape, mybir.dt.from_np(a.dtype), kind="ExternalInput").ap())
    out = nc.dram_tensor("out_0_dram", inputs["x"].shape, F32, kind="ExternalOutput").ap()
    gcn_three_layers_resnorm(nc, *aps, out)
    result = run_bass_kernel_spmd(nc, [arrays], core_ids=[0])
    return result.results[0]["out_0_dram"]
```
